# Optimizing a Trainium2 kernel written in Bass

```python
import numpy as np
import jax
import jax.numpy as jnp

def _softmax(x, axis=-1):
    return jax.nn.softmax(x, axis=axis)

def _gelu(x):
    return jax.nn.gelu(x, approximate=True)

def _silu(x):
    return jax.nn.silu(x)

def _sigmoid(x):
    return jax.nn.sigmoid(x)

def _layernorm(x, axis=-1, eps=1e-05):
    m = jnp.mean(x, axis=axis, keepdims=True)
    v = jnp.var(x, axis=axis, keepdims=True)
    return (x - m) / jnp.sqrt(v + eps)

def _scatter_add(tgt, idx, src, axis=0):
    return tgt.at[idx].add(src)

def _segment_sum(src, seg, n):
    return jax.ops.segment_sum(src, seg, n)
kernel_name = 'mk_gnn_preln_d1_gnn_r8_42dbf4'

def setup_inputs(seed: int=0):
    np.random.seed(seed)
    _w = jnp.asarray

    def _rec_inputs():
        import jax
        import jax.numpy as jnp
        _gk = jax.random.key(seed)
        x = -0.0003713 + 1 * jax.random.normal(jax.random.fold_in(_gk, 1), (12500, 128), jnp.float32)
        src = jax.random.randint(jax.random.fold_in(_gk, 2), (200000,), 0, 12500, jnp.int32)
        dst = jax.random.randint(jax.random.fold_in(_gk, 3), (200000,), 0, 12500, jnp.int32)
        _o = jnp.argsort(dst, stable=True)
        src = src[_o]
        dst = dst[_o]
        edge_weight = jax.random.uniform(jax.random.fold_in(_gk, 12), (200000,), jnp.float32, 0.0, 0.999999)
        return (x, src, dst, edge_weight)
    x, src, dst, edge_weight = _rec_inputs()

    def _L0_gnn_setup():
        import jax
        import jax.numpy as jnp
        import numpy as np
        N = 12500
        D = 128
        M = 200000
        TOPK = 16
        DECAY_LAMBDA = 1.0
        key = jax.random.key(seed)
        ks = jax.random.split(key, 7)
        scale = 1.0 / np.sqrt(D)
        return {'node_feats': jax.random.normal(ks[0], (N, D), jnp.float32), 'edge_index': jax.random.randint(ks[1], (2, M), 0, N, dtype=jnp.int64), 'edge_dt': jax.random.uniform(ks[2], (M,), jnp.float32), 'W_self': jax.random.normal(ks[3], (D, D), jnp.float32) * scale, 'W_msg': jax.random.normal(ks[4], (D, D), jnp.float32) * scale, 'W_Q': jax.random.normal(ks[5], (D, D), jnp.float32) * scale, 'W_K': jax.random.normal(ks[6], (D, D), jnp.float32) * scale}
    _L0_gnn_all = _L0_gnn_setup()
    _L0_gnn_in = {k: v for k, v in _L0_gnn_all.items() if k in ('W_self', 'W_msg', 'W_Q', 'W_K')}
    del _L0_gnn_all
    return {'x': x, 'src': src, 'dst': dst, 'edge_weight': edge_weight, 'L0_gnn_W_self': _L0_gnn_in['W_self'], 'L0_gnn_W_msg': _L0_gnn_in['W_msg'], 'L0_gnn_W_Q': _L0_gnn_in['W_Q'], 'L0_gnn_W_K': _L0_gnn_in['W_K']}

def reference(x, src, dst, edge_weight, L0_gnn_W_self, L0_gnn_W_msg, L0_gnn_W_Q, L0_gnn_W_K):
    import jax
    import jax.numpy as jnp

    def _L0_gnn_ref(node_feats, edge_index, edge_dt, W_self, W_msg, W_Q, W_K):
        import jax
        import jax.numpy as jnp
        import numpy as np
        N = 12500
        D = 128
        M = 200000
        TOPK = 16
        DECAY_LAMBDA = 1.0
        n, d = node_feats.shape
        src, dst = (edge_index[0], edge_index[1])
        Qv = node_feats @ W_Q.T
        Ku = node_feats @ W_K.T
        score = jnp.einsum('md,md->m', Qv[dst], Ku[src]) * (1.0 / np.sqrt(d))
        score = score * jnp.exp(-DECAY_LAMBDA * edge_dt)
        order = jnp.lexsort((-score, dst))
        dst_s = dst[order]
        src_s = src[order]
        score_s = score[order]
        seg_start = jnp.searchsorted(dst_s, dst_s, side='left')
        rank = jnp.arange(dst_s.shape[0]) - seg_start
        keep = rank < TOPK
        neg_inf = jnp.float32(-jnp.inf)
        score_m = jnp.where(keep, score_s, neg_inf)
        seg_max = jax.ops.segment_max(score_m, dst_s, num_segments=n, indices_are_sorted=True)
        w = jnp.where(keep, jnp.exp(score_m - seg_max[dst_s]), 0.0)
        denom = jax.ops.segment_sum(w, dst_s, num_segments=n, indices_are_sorted=True)
        alpha = w / jnp.where(denom[dst_s] > 0, denom[dst_s], 1.0)
        msgs = node_feats[src_s] @ W_msg.T
        agg = jax.ops.segment_sum(alpha[:, None] * msgs, dst_s, num_segments=n, indices_are_sorted=True)
        return jax.nn.relu(node_feats @ W_self.T + agg)
    edge_index = jnp.stack([src, dst])
    h = jnp.maximum(_layernorm(x, axis=-1), 0.0)
    x = x + _L0_gnn_ref(h, edge_index, edge_weight, L0_gnn_W_self, L0_gnn_W_msg, L0_gnn_W_Q, L0_gnn_W_K)
    return x

_drawn_inputs = setup_inputs


def setup_inputs(seed=0):
    import zlib

    import numpy as np

    out = dict(_drawn_inputs(seed))
    spreads = {}
    factors = {}
    for name, (base, spread) in spreads.items():
        noise = np.random.default_rng([zlib.crc32(name.encode()), seed]).standard_normal(out[name].shape)
        drawn = base * np.exp(spread * noise) if base else spread * noise
        out[name] = jnp.asarray(drawn.astype(out[name].dtype))
    for name, factor in factors.items():
        out[name] = (out[name] * factor).astype(out[name].dtype)
    return out
```

```python
import concourse.bass as bass
from concourse import mybir
from contextlib import ExitStack


class Line:

    def __init__(self, sem, names):
        self.sem, self.names = sem, names
        self.done = 0

    def mark(self, ins, b, name):
        at = b * len(self.names) + self.names.index(name)
        assert at == self.done, (b, name, self.done)
        self.done += 1
        ins.then_inc(self.sem, 1)

    def wait(self, eng, b, name):
        if b >= 0:
            eng.wait_ge(self.sem, b * len(self.names) + self.names.index(name) + 1)


def gnn_kernel(nc, x, src, dst, ew, w_self, w_msg, w_q, w_k, out):
    f32, i32, bf16, i16 = mybir.dt.float32, mybir.dt.int32, mybir.dt.bfloat16, mybir.dt.int16
    ALU, ACT, AX = mybir.AluOpType, mybir.ActivationFunctionType, mybir.AxisListType

    N, D, M = 12500, 128, 200000
    NB, B = 125, 100
    T, TP, SLOT = 17, 18, 48
    DC = 3 * SLOT + 1
    CAP = T * 128
    RUN = 1600
    NR = M // RUN
    MP = M + CAP
    ROWS = 98
    SCALE = 1.0 / D ** 0.5
    NEG = -3.0e38
    TAKEN = -3.4e38
    CUT = -3.2e38
    EPS = 1e-5
    GG = [4, 4, 4, 4, 1]
    GW = [9, 8]
    GP = [5, 4, 4, 4]
    CH = 14
    NCH = ROWS // CH

    H = nc.dram_tensor("H_table", [N, D], f32, kind="Internal").ap()
    D16 = nc.dram_tensor("D16_table", [1, MP], i16, kind="Internal").ap()
    META = nc.dram_tensor("META_table", [4, MP], f32, kind="Internal").ap()

    ctx = ExitStack()
    with ctx:
        def sb(name, shape, dt=f32):
            return ctx.enter_context(nc.sbuf_tensor(name, shape, dt))

        def pb(name):
            return ctx.enter_context(nc.psum_tensor(name, [128, 512], f32))

        def sem(name):
            return ctx.enter_context(nc.semaphore(name))

        iota = sb("iota", [128, 128])
        pidx = sb("pidx", [128, 1])
        ident = sb("ident", [128, 128])
        boff = sb("boff", [128, B])
        boffp = sb("boffp", [128, B])
        iotaN = sb("iotaN", [128, NB, TP], bf16)
        iotaJ = sb("iotaJ", [128, SLOT, TP], bf16)
        thr = sb("thr", [128, 1])
        ones = sb("ones", [128, 1])
        wts = sb("wts", [128, 4, 128])
        A = sb("A", [128, 128])
        WsT = sb("WsT", [128, 128])
        WmT = sb("WmT", [128, 128])
        zc = sb("zc", [128, 1])
        epsc = sb("epsc", [128, 1])

        X = sb("X", [128, ROWS, 128])
        st6 = sb("st6", [128, ROWS, 6])
        mean = sb("mean", [128, ROWS])
        dif = sb("dif", [128, ROWS])
        var = sb("var", [128, ROWS])
        rstd = sb("rstd", [128, ROWS])
        nmr = sb("nmr", [128, ROWS])

        rawi = sb("rawi", [NR, RUN + 1], i32)
        rawd = sb("rawd", [NR, RUN + 1])
        ewt = sb("ewt", [NR, RUN])
        stt = sb("stt", [NR, RUN])
        carry = sb("carry", [NR, 1])
        cmask = sb("cmask", [NR, NR])
        ctmp = sb("ctmp", [NR, NR])
        pad = sb("pad", [4, CAP])
        pad16 = sb("pad16", [1, CAP], i16)
        dst16 = sb("dst16", [NR, RUN], i16)
        cnt1 = sb("cnt1", [128, 1])
        win = sb("win", [128, 1])
        wini = sb("wini", [128, 1], i32)
        cnt2 = sb("cnt2", [128, 1])
        rb = sb("rb", [128, 1])
        rbrow = sb("rbrow", [1, 128], i32)
        rbf = sb("rbf", [1, 128])

        MR = [sb(f"MR{q}", [128, 128]) for q in range(2)]
        dec_ = [sb(f"dec{q}", [128, TP]) for q in range(3)]
        slb = [sb(f"slb{q}", [128, TP], bf16) for q in range(3)]
        dlb = [sb(f"dlb{q}", [128, TP], bf16) for q in range(3)]
        idx = [sb(f"idx{q}", [128, TP], i32) for q in range(3)]
        dB = [sb(f"dB{q}", [128, T * 128], i16) for q in range(2)]
        hb = [sb(f"hb{q}", [128, 128]) for q in range(2)]
        xb = [sb(f"xb{q}", [128, 128]) for q in range(2)]
        hT = [sb(f"hT{q}", [128, 128]) for q in range(2)]
        G3 = [sb(f"G3{q}", [128, 3, 128], bf16) for q in range(2)]
        Gr = sb("Gr", [128, 128])
        Et = [sb(f"E{q}", [128, T * 128]) for q in range(3)]
        OT = [sb(f"OT{q}", [128, NB, TP], bf16) for q in range(2)]
        O = [sb(f"O{q}", [128, T * 128], bf16) for q in range(2)]
        P = sb("P", [128, T * 128])
        D01 = [sb(f"D01{q}", [128, SLOT, TP], bf16) for q in range(2)]
        Dm = sb("Dm", [128, DC, TP], bf16)
        junk = sb("junk", [128, T * 128])
        dect = sb("dect", [NR, RUN])
        eid, neq, dec = Et[0][0:NR, 0:RUN], Et[1][0:NR, 0:RUN], dect[:, :]
        srcf = Et[2][0:NR, 0:RUN]
        srci = srcf.bitcast(i32)
        wrun, wjunk = P[:, 0:RUN].bitcast(i32), junk[:, 0:RUN]
        s = sb("s", [128, TP])
        sd = sb("sd", [128, TP])
        s3 = sb("s3", [128, 3, TP], bf16)
        sr = sb("sr", [128, 2, TP])
        w = sb("w", [128, TP])
        jw = sb("jw", [128, T, SLOT])
        DEG = sb("DEG", [128, B])
        pen = sb("pen", [128, SLOT])
        Sm = sb("Sm", [128, SLOT])
        S2 = sb("S2", [128, SLOT])
        S3 = sb("S3", [128, SLOT])
        v8 = sb("v8", [128, 16])
        neg = sb("neg", [128, 1])
        ex = sb("ex", [128, SLOT])
        wk = sb("wk", [128, SLOT])
        den = sb("den", [128, 1])
        rden = sb("rden", [128, 1])
        W = sb("W", [128, SLOT])
        Wr = sb("Wr", [128, SLOT])
        W3 = sb("W3", [128, 3, SLOT], bf16)
        Us = sb("Us", [128, 128])
        ob = [sb(f"ob{q}", [128, 128]) for q in range(2)]

        hot = X[:, 16, 0:B]
        hrow = X[0:1, 17:21, :].rearrange("p a b -> p (a b)")
        hint = sb("hint", [1, B + 1], i32)
        bcol = sb("bcol", [128, 1])
        FM = sb("FM", [128, 4])
        fidx = sb("fidx", [128, 1], i32)
        fdl = sb("fdl", [128, 1])
        fs = sb("fs", [128, 2])
        tie = sb("tie", [128, 4])
        FE, FOT, FO, GF, DG, FW, FP, UA, EQ, KP, CU = (X[:, k, :] for k in range(11))
        C1, C2 = X[:, 12:14, :].rearrange("p a b -> p (a b)"), X[:, 14:16, :].rearrange("p a b -> p (a b)")
        FC = 16 + 128

        pA = pb("pA")
        pB = pb("pB")
        pG = [pb(f"pG{g}") for g in range(4)]
        pS = pb("pS")
        pU = pb("pU")
        pO = pU[:, 128:256]

        s_x = [sem(f"s_x{c}") for c in range(NCH)]
        s_w = sem("s_w")
        s_dst = sem("s_dst")
        s_src = sem("s_src")
        s_ew = sem("s_ew")
        s_io = sem("s_io")
        s_v = sem("s_v")
        s_a = sem("s_a")
        s_p = sem("s_p")
        s_run = sem("s_run")
        s_ht = sem("s_ht")
        s_mt = sem("s_mt")
        s_mr = [sem(f"s_mr{q}") for q in range(2)]
        s_db = [sem(f"s_db{q}") for q in range(2)]
        s_hb = [sem(f"s_hb{q}") for q in range(2)]
        s_xb = [sem(f"s_xb{q}") for q in range(2)]
        s_st = [sem(f"s_st{q}") for q in range(2)]
        s_g = [sem(f"s_g{q}") for q in range(2)]
        s_er = sem("s_er")
        s_relay = sem("s_relay")
        s_fl = sem("s_fl")
        s_fg = sem("s_fg")
        s_tick = sem("s_tick")

        SEL = ["deg", "pen", "Sh", "Shm", "Sm", "m8a", "neg", "mr1", "m8b", "mr2", "keep", "rec", "W", "Wh", "Wr", "Wm", "Wl"]
        VM = Line(sem("VM"), [f"s{g}" for g in range(5)] + ["sd", "sh", "sr", "sm", "sr2", "sl", "D"] + SEL
                  + ["jw0", "w0", "jw1", "w1"])
        VF = Line(sem("VF"), ["fin"])
        VA = Line(sem("VA"), ["idx", "M"])
        VB = Line(sem("VB"), ["D01", "O", "Gr", "OT", "Gl"])
        PG = Line(sem("PG"), ["Gx2", "Gx3", "Gx0", "Gx1", "Gx4"])
        PM = Line(sem("PM"), ["Sc", "Wx0", "Wx1", "agg0", "agg1", "agg2", "agg3", "out"])
        PA = Line(sem("PA"), ["mT"])
        PB = Line(sem("PB"), ["hT", "G"])
        AM = Line(sem("AM"), ["exp", "P0", "P1", "P2", "P3", "U"])
        AB = Line(sem("AB"), ["hT", "Gh", "Gm"])

        g0 = [sum(GG[:g]) for g in range(5)]
        w0 = [sum(GW[:g]) for g in range(2)]
        p0 = [sum(GP[:g]) for g in range(4)]

        class Once:

            def __init__(self, sm, names):
                self.sem, self.names, self.done = sm, names, 0

            def mark(self, ins, name):
                assert self.names[self.done] == name, (name, self.names[self.done])
                self.done += 1
                ins.then_inc(self.sem, 1)

            def wait(self, eng, name):
                eng.wait_ge(self.sem, self.names.index(name) + 1)

        vn = ["zero", "ident", "mr0", "rawd", "neq", "val", "scan", "c1", "winr", "win", "wini",
              "ctmp", "carry", "stt", "slot", "cnt2", "rb", "rbrow", "rbf"]
        for c in range(NCH):
            vn += [f"{k}{c}" for k in ("bn", "sum", "dif", "mean", "sq", "m2", "var", "rstd", "nmr")]
        VS = Once(s_v, vn)
        AS = Once(s_a, ["dec", "d16", "srcf", "A", "WsT", "WmT"] + [f"{k}{c}" for c in range(NCH) for k in ("sq", "h")])
        PS = Once(s_p, ["smp", "A", "WsT", "WmT", "last", "rb"])
        IO = Once(s_io, ["iota", "pidx", "boff", "boffp", "thr", "eid", "cmask", "pad", "pad16", "iotaN", "iotaJ"])

        xr = x[0:127 * ROWS, :].rearrange("(p r) d -> p r d", r=ROWS)
        hr = H[0:127 * ROWS, :].rearrange("(p r) d -> p r d", r=ROWS)
        tail = N - ROWS
        first = 127 * ROWS - tail
        dst2 = dst.rearrange("(p r) -> p r", r=RUN)
        src2 = src.rearrange("(p r) -> p r", r=RUN)
        ew2 = ew.rearrange("(p r) -> p r", r=RUN)
        PARTS = [(0, 112), (112, 127)]

        R_ = slice(0, NB)

        def step(engine, fn, dmas=0):
            return ("step", engine, fn, dmas)

        def repeat(kind, steps):
            return (kind, None, steps, 0)

        def fetch(e, v):
            for k in (0, 1, 3):
                last = e.dma_start(FM[:, k:k + 1], META[k, bass.ds(v["e0"], 128)].rearrange("(p a) -> p a", a=1),
                                   allow_slow_non_contiguous=True).then_inc(s_fl, 16)
            return last

        SCORES = [
            step("SP", fetch, 3),
            step("DVE", lambda e, v: (e.tensor_copy(fidx[:, :], FM[:, 0:1]),
                                      e.tensor_tensor(fdl[:, :], FM[:, 1:2], bcol[:, :], ALU.subtract))[-1]),
            step("Pool", lambda e, v: e.indirect_dma_start(
                out=FE, out_offset=None, in_=H,
                in_offset=bass.IndirectOffsetOnAxis(ap=fidx[:, 0:1], axis=0)).then_inc(s_fg, 16), 1),
            step("DVE", lambda e, v: e.tensor_scalar(FOT, iota[:, :], fdl[:, 0:1], None, ALU.is_equal)),
            step("PE", lambda e, v: e.transpose(pA[R_, 0:128], FOT[:, R_], ident[:, :])),
            step("ACT", lambda e, v: e.activation(FO[R_, :], pA[R_, 0:128], ACT.Copy)),
            step("PE", lambda e, v: e.matmul(pB[:, 0:128], lhsT=FO[R_, :], rhs=GF[R_, :], start=True, stop=True)),
            step("DVE", lambda e, v: e.tensor_tensor_reduce(out=DG, in0=FE, in1=pB[:, 0:128], scale=1.0, scalar=0.0,
                                                            op0=ALU.mult, op1=ALU.add, accum_out=fs[:, 0:1])),
            step("DVE", lambda e, v: e.tensor_tensor(fs[:, 1:2], fs[:, 0:1], FM[:, 3:4], ALU.mult)),
            step("DVE", lambda e, v: e.tensor_scalar(DG, ident[:, :], fs[:, 1:2], None, ALU.mult)),
            step("PE", lambda e, v: e.matmul(pS[R_, 0:128], lhsT=FOT[:, R_], rhs=DG, start=True, stop=True)),
            step("DVE", lambda e, v: e.tensor_scalar(EQ[R_, :], FO[R_, :], 1.0, -NEG, ALU.subtract, ALU.mult)),
            step("DVE", lambda e, v: e.tensor_tensor(C1[R_, 16:FC], pS[R_, 0:128], EQ[R_, :], ALU.add)),
        ]
        BEST = [
            step("DVE", lambda e, v: e.max(v8[R_, 0:8], C1[R_, 0:FC])),
            step("DVE", lambda e, v: e.match_replace(C2[R_, 0:FC], v8[R_, 0:8], C1[R_, 0:FC], TAKEN)),
            step("DVE", lambda e, v: e.max(v8[R_, 8:16], C2[R_, 0:FC])),
            step("DVE", lambda e, v: e.tensor_copy(C1[R_, 0:16], v8[R_, 0:16])),
        ]
        MIX = [
            step("DVE", lambda e, v: (e.tensor_scalar(EQ[R_, :], C1[R_, 16:FC], v8[R_, 15:16], None, ALU.is_equal),
                                      e.tensor_scalar(KP[R_, :], C1[R_, 16:FC], v8[R_, 15:16], None, ALU.is_gt))[-1]),
            step("DVE", lambda e, v: e.tensor_tensor_scan(CU[R_, :], EQ[R_, :], EQ[R_, :], tie[R_, 0:1], ALU.add, ALU.max)),
            step("DVE", lambda e, v: e.tensor_copy(tie[R_, 0:1], CU[R_, 127:128])),
            step("DVE", lambda e, v: e.scalar_tensor_tensor(EQ[R_, :], CU[R_, :], tie[R_, 1:2], EQ[R_, :], ALU.is_le, ALU.mult)),
            step("DVE", lambda e, v: e.tensor_tensor(KP[R_, :], KP[R_, :], EQ[R_, :], ALU.add)),
            step("ACT", lambda e, v: e.activation(FW[R_, :], C1[R_, 16:FC], ACT.Exp, bias=neg[R_, :])),
            step("DVE", lambda e, v: e.scalar_tensor_tensor(FW[R_, :], FW[R_, :], rden[R_, 0:1], KP[R_, :], ALU.mult, ALU.mult)),
            step("PE", lambda e, v: e.transpose(pB[:, R_], FW[R_, :], ident[R_, R_])),
            step("ACT", lambda e, v: e.activation(FP[:, R_], pB[:, R_], ACT.Copy)),
            step("PE", lambda e, v: e.matmul(pU[:, R_], lhsT=FE, rhs=FP[:, R_], start=True, stop=True)),
            step("DVE", lambda e, v: e.tensor_tensor(UA[:, R_], UA[:, R_], pU[:, R_], ALU.add)),
        ]
        HEAVY = [
            step("SP", lambda e, v: (e.dma_start(hb[0][R_, :], H[bass.ds(v["b"] * NB, NB), :]).then_inc(s_fl, 16),
                                     e.dma_start(xb[0][R_, :], x[bass.ds(v["b"] * NB, NB), :]).then_inc(s_fl, 16)), 2),
            step("DVE", lambda e, v: (e.memset(UA, 0.0), e.memset(C1[:, 0:16], NEG), e.memset(tie[:, 0:1], 0.0),
                                      e.tensor_copy(bcol[:, :], boff[:, bass.ds(v["b"], 1)]))[-1]),
            step("PE", lambda e, v: e.transpose(pB[:, R_], hb[0][R_, :], ident[R_, R_])),
            step("ACT", lambda e, v: e.activation(hT[0][:, R_], pB[:, R_], ACT.Copy)),
            step("PE", lambda e, v: e.matmul(pA[R_, 0:128], lhsT=hT[0][:, R_], rhs=A[:, :], start=True, stop=True)),
            step("ACT", lambda e, v: e.activation(GF[R_, :], pA[R_, 0:128], ACT.Copy)),
            repeat("edges", SCORES + BEST),
            step("DVE", lambda e, v: e.tensor_scalar(neg[R_, :], v8[R_, 0:1], -1.0, None, ALU.mult)),
            step("ACT", lambda e, v: e.activation(ex[R_, 0:16], v8[R_, 0:16], ACT.Exp, bias=neg[R_, :])),
            step("DVE", lambda e, v: e.tensor_scalar(wk[R_, 0:16], v8[R_, 0:16], v8[R_, 15:16], None, ALU.is_equal)),
            step("DVE", lambda e, v: e.tensor_reduce(tie[R_, 1:2], wk[R_, 0:16], AX.X, ALU.add)),
            step("DVE", lambda e, v: e.tensor_reduce(den[R_, :], ex[R_, 0:16], AX.X, ALU.add)),
            step("DVE", lambda e, v: e.reciprocal(rden[R_, :], den[R_, :])),
            repeat("edges", SCORES + MIX),
            step("PE", lambda e, v: (e.matmul(pO[R_, :], lhsT=hT[0][:, R_], rhs=WsT[:, :], start=True, stop=False),
                                     e.matmul(pO[R_, :], lhsT=UA[:, R_], rhs=WmT[:, :], start=False, stop=True))[-1]),
            step("DVE", lambda e, v: e.scalar_tensor_tensor(ob[0][R_, :], pO[R_, :], 0.0, xb[0][R_, :], ALU.max, ALU.add)),
            step("SP", lambda e, v: e.dma_start(out[bass.ds(v["b"] * NB, NB), :], ob[0][R_, :]).then_inc(s_fl, 16), 1),
        ]
        FLAGS = [
            step("DVE", lambda e, v: e.tensor_scalar(hot[R_, :], DEG[R_, :], float(SLOT), None, ALU.is_gt)),
            step("PE", lambda e, v: e.matmul(pS[0:1, 0:B], lhsT=ones[R_, :], rhs=hot[R_, :], start=True, stop=True)),
            step("DVE", lambda e, v: (e.tensor_scalar(hrow[:, 0:B], pS[0:1, 0:B], 0.0, None, ALU.is_gt),
                                      e.tensor_tensor(hrow[:, B:2 * B], rbf[0:1, 1:B + 1], rbf[0:1, 0:B], ALU.subtract))[-1]),
            step("DVE", lambda e, v: e.scalar_tensor_tensor(hrow[:, 2 * B:3 * B], hrow[:, B:2 * B], float(CAP),
                                                            hrow[:, 0:B], ALU.is_gt, ALU.max)),
            step("DVE", lambda e, v: e.tensor_reduce(hrow[:, 3 * B:3 * B + 1], hrow[:, 2 * B:3 * B], AX.X, ALU.add)),
            step("DVE", lambda e, v: (e.tensor_copy(hint[:, 0:B], hrow[:, 2 * B:3 * B]),
                                      e.tensor_copy(hint[:, B:B + 1], hrow[:, 3 * B:3 * B + 1]))[-1]),
        ]

        def general(eng, me):
            place, mine = eng.alloc_register(f"place_{me}"), eng.alloc_register(f"mine_{me}")
            eng.reg_mov(place, 1)
            eng.reg_mov(mine, 0)
            v = {}

            def held(sm, value):
                eng.wait_ge(sm, value)
                eng.sem_inc(s_tick, 1)

            def walk(steps):
                behind = 0
                for kind, engine, what, dmas in steps:
                    if kind == "edges":
                        eng.reg_add(place, place, behind)
                        behind = 0
                        with eng.Fori(v["r0"], v["r1"], 128) as e0:
                            v["e0"] = e0
                            walk(what)
                        continue
                    if engine == me:
                        if behind:
                            eng.reg_add(place, place, behind)
                        behind = 0
                        held(s_relay, place)
                        ins = what(eng, v)
                        if dmas > 0:
                            eng.reg_add(mine, mine, 16 * dmas)
                            held(s_fl if me == "SP" else s_fg, mine)
                            eng.sem_inc(s_relay, 1)
                        else:
                            ins.then_inc(s_relay, 1)
                    behind += 1
                if behind:
                    eng.reg_add(place, place, behind)

            walk(FLAGS)
            held(s_relay, place)
            some = eng.value_load(hint[0:1, B:B + 1], min_val=0, max_val=B)
            with eng.If(some > 0):
                with eng.Fori(0, B) as b:
                    v["b"] = b
                    this = eng.value_load(hint[0:1, bass.ds(b, 1)], min_val=0, max_val=1)
                    with eng.If(this > 0):
                        v["r0"] = eng.value_load(rbrow[0:1, bass.ds(b, 1)], min_val=0, max_val=M)
                        v["r1"] = eng.value_load(rbrow[0:1, bass.ds(b + 1, 1)], min_val=0, max_val=M)
                        walk(HEAVY)

        block = ctx.enter_context(nc.Block())

        @block.sync
        def _(eng):
            eng.dma_start(rawi[:, 1:], dst2).then_inc(s_dst, 16)
            eng.dma_start(rawi[1:NR, 0:1], dst2[0:NR - 1, RUN - 1:RUN], allow_slow_non_contiguous=True).then_inc(s_dst, 16)
            for c in range(NCH):
                a, z = c * CH, (c + 1) * CH
                for p, q in PARTS:
                    eng.dma_start(X[p:q, a:z, :], xr[p:q, a:z, :]).then_inc(s_x[c], 16)
                eng.dma_start(X[127:128, a:z, :], x[tail + a:tail + z, :].rearrange("(p r) d -> p r d", p=1)).then_inc(s_x[c], 16)
                if c == 0:
                    eng.dma_start(ewt[:, :], ew2).then_inc(s_ew, 16)
                    eng.dma_start(srci, src2).then_inc(s_src, 16)
                    for k, wt in enumerate((w_q, w_k, w_self, w_msg)):
                        eng.dma_start(wts[:, k, :], wt).then_inc(s_w, 16)

            def put(row, tile):
                eng.dma_start(META[row, 0:M].rearrange("(p r) -> p r", r=RUN), tile).then_inc(s_mt, 16)

            IO.wait(eng, "pad16")
            eng.dma_start(D16[0:1, M:MP], pad16[:, :]).then_inc(s_mt, 16)
            eng.dma_start(META[0:4, M:MP], pad[:, :]).then_inc(s_mt, 16)
            VS.wait(eng, "rawd")
            eng.dma_start(META[1, 0:M].rearrange("(p r) -> p r", r=RUN), rawd[:, 1:]).then_inc(s_mt, 16)
            AS.wait(eng, "dec")
            put(3, dec)
            AS.wait(eng, "d16")
            eng.dma_start(D16[0, 0:M].rearrange("(p r) -> p r", r=RUN), dst16[:, :]).then_inc(s_mt, 16)
            AS.wait(eng, "srcf")
            put(0, srcf)
            VS.wait(eng, "slot")
            put(2, stt[:, :])
            for c in range(NCH):
                a, z = c * CH, (c + 1) * CH
                AS.wait(eng, f"h{c}")
                for p, q in PARTS:
                    eng.dma_start(hr[p:q, a:z, :], X[p:q, a:z, :]).then_inc(s_ht, 16)
                lo = max(a, first)
                if lo < z:
                    eng.dma_start(H[tail + lo:tail + z, :].rearrange("(p r) d -> p r d", p=1), X[127:128, lo:z, :]).then_inc(s_ht, 16)

            VS.wait(eng, "rbf")
            eng.wait_ge(s_mt, 16 * 7)

            def meta(b):
                q = b % 2
                if b >= 2:
                    PA.wait(eng, b - 2, "mT")
                r = eng.value_load(rbrow[0:1, b:b + 1], min_val=0, max_val=M)
                for k in range(4):
                    eng.dma_start(MR[q][32 * k:32 * k + T, :],
                                  META[k, bass.ds(r, CAP)].rearrange("(t e) -> t e", e=128)).then_inc(s_mr[q], 16)
                VB.wait(eng, b - 2, "O")
                eng.dma_start(dB[q][:, :], D16[0:1, bass.ds(r, CAP)].to_broadcast([128, CAP])).then_inc(s_db[q], 16)

            def load_h(b):
                q = b % 2
                PB.wait(eng, b - 2, "hT")
                eng.dma_start(hb[q][0:NB, :], H[b * NB:(b + 1) * NB, :]).then_inc(s_hb[q], 16)

            def load_x(b):
                q = b % 2
                VF.wait(eng, b - 2, "fin")
                eng.dma_start(xb[q][0:NB, :], x[b * NB:(b + 1) * NB, :]).then_inc(s_xb[q], 16)

            VS.wait(eng, "mr0")
            for b in range(3):
                if b < 2:
                    meta(b)
            nht = sum(2 + (max(c * CH, first) < (c + 1) * CH) for c in range(NCH))
            eng.wait_ge(s_ht, 16 * nht)
            meta(2)
            load_h(0)
            load_h(1)
            load_x(0)
            for j in range(B):
                if j + 3 < B:
                    meta(j + 3)
                if j + 2 < B:
                    load_h(j + 2)
                if j + 1 < B:
                    load_x(j + 1)
                if j >= 1:
                    VF.wait(eng, j - 1, "fin")
                    eng.dma_start(out[(j - 1) * NB:j * NB, :], ob[(j - 1) % 2][0:NB, :]).then_inc(s_st[(j - 1) % 2], 16)
            VF.wait(eng, B - 1, "fin")
            eng.dma_start(out[(B - 1) * NB:B * NB, :], ob[(B - 1) % 2][0:NB, :]).then_inc(s_st[(B - 1) % 2], 16)
            eng.wait_ge(s_st[0], 16 * (B // 2))
            eng.wait_ge(s_st[1], 16 * (B // 2))
            eng.sem_inc(s_relay, 1)
            general(eng, "SP")

        @block.gpsimd
        def _(eng):
            small = dict(allow_small_or_imprecise_dtypes=True)
            IO.mark(eng.iota(iota[:, :], pattern=[[1, 128]], base=0, channel_multiplier=0, **small), "iota")
            IO.mark(eng.iota(pidx[:, :], pattern=[[0, 1]], base=0, channel_multiplier=1, **small), "pidx")
            IO.mark(eng.iota(boff[:, :], pattern=[[NB, B]], base=0, channel_multiplier=0, **small), "boff")
            IO.mark(eng.iota(boffp[:, :], pattern=[[NB, B]], base=0, channel_multiplier=1, **small), "boffp")
            IO.mark(eng.iota(thr[:, :], pattern=[[0, 1]], base=0, channel_multiplier=NB, **small), "thr")
            IO.mark(eng.iota(eid, pattern=[[1, RUN]], base=0, channel_multiplier=RUN, **small), "eid")
            IO.mark(eng.iota(cmask[:, :], pattern=[[-1, NR]], base=0, channel_multiplier=1, **small), "cmask")
            IO.mark(eng.iota(pad[:, :], pattern=[[0, CAP]], base=0, channel_multiplier=-1, **small), "pad")
            IO.mark(eng.iota(pad16[:, :], pattern=[[0, CAP]], base=-1, channel_multiplier=0, **small), "pad16")
            IO.mark(eng.iota(iotaN[:, :, :], pattern=[[1, NB], [0, TP]], base=0, channel_multiplier=0, **small), "iotaN")
            IO.mark(eng.iota(iotaJ[:, :, :], pattern=[[1, SLOT], [0, TP]], base=0, channel_multiplier=0, **small), "iotaJ")
            VS.wait(eng, "wini")
            eng.indirect_dma_start(out=wrun, out_offset=None, in_=dst2,
                                   in_offset=bass.IndirectOffsetOnAxis(ap=wini[:, 0:1], axis=0)).then_inc(s_run, 16)
            VS.wait(eng, "rbrow")
            VS.wait(eng, "zero")
            nht = sum(2 + (max(c * CH, first) < (c + 1) * CH) for c in range(NCH))
            eng.wait_ge(s_ht, 16 * nht)

            def gather(b, t):
                q = b % 3
                return eng.indirect_dma_start(
                    out=Et[q][:, t * 128:(t + 1) * 128], out_offset=None, in_=H,
                    in_offset=bass.IndirectOffsetOnAxis(ap=idx[q][:, t:t + 1], axis=0)).then_inc(s_g[b % 2], 16)

            total = [eng.alloc_register(f"total{q}") for q in range(2)]
            for q in range(2):
                eng.reg_mov(total[q], 0)

            def arrived(b):
                eng.wait_ge(s_g[b % 2], total[b % 2])
                eng.sem_inc(s_er, 1)

            for b in range(B):
                q = b % 2
                VA.wait(eng, b, "idx")
                PM.wait(eng, b - 3, "agg3")
                r0 = eng.value_load(rbrow[0:1, b:b + 1], min_val=0, max_val=M)
                r1 = eng.value_load(rbrow[0:1, b + 1:b + 2], min_val=0, max_val=M)
                n = eng.snap(r1 - r0, min_val=0, max_val=M)
                for t in range(16):
                    gather(b, t)
                    if t == 3 and b > 0:
                        arrived(b - 1)
                eng.reg_add(total[q], total[q], 16 * 16)
                for t in range(16, T):
                    with eng.If(n > t * 128):
                        gather(b, t)
                        eng.reg_add(total[q], total[q], 16)
            arrived(B - 1)
            general(eng, "Pool")

        @block.vector
        def _(eng):
            for q in range(3):
                eng.memset(Et[q][:, 16 * 128:], 0.0)
            eng.memset(zc[:, :], 0.0)
            eng.memset(epsc[:, :], EPS)
            eng.memset(ones[:, :], 1.0)
            eng.memset(s[:, :], 0.0)
            eng.memset(Dm[:, 3 * SLOT, :], 1.0)
            VS.mark(eng.memset(rawi[0:1, 0:1], -1), "zero")
            IO.wait(eng, "pidx")
            VS.mark(eng.tensor_scalar(ident[:, :], iota[:, :], pidx[:, 0:1], None, ALU.is_equal), "ident")
            eng.memset(MR[0][:, :], 0.0)
            VS.mark(eng.memset(MR[1][:, :], 0.0), "mr0")
            eng.wait_ge(s_dst, 32)
            VS.wait(eng, "zero")
            VS.mark(eng.tensor_copy(rawd[:, :], rawi[:, :]), "rawd")
            VS.wait(eng, "rawd")
            VS.mark(eng.tensor_tensor(neq, rawd[:, 1:], rawd[:, 0:RUN], ALU.not_equal), "neq")
            VS.wait(eng, "neq")
            IO.wait(eng, "cmask")
            VS.mark(eng.tensor_tensor(neq, neq, eid, ALU.mult), "val")
            VS.wait(eng, "val")
            VS.mark(eng.tensor_tensor_scan(stt[:, :], neq, neq, 0.0, ALU.max, ALU.max), "scan")
            PS.wait(eng, "smp")
            VS.mark(eng.tensor_scalar(wjunk[:, 0:NR], pG[0][:, 0:NR], thr[:, 0:1], 0.0, ALU.is_lt, ALU.add,
                                      accum_out=cnt1[:, :]), "c1")
            VS.wait(eng, "c1")
            VS.mark(eng.tensor_scalar(win[:, :], cnt1[:, :], -1.0, 0.0, ALU.add, ALU.max), "winr")
            VS.wait(eng, "winr")
            VS.mark(eng.tensor_scalar(rb[:, :], win[:, :], float(RUN), None, ALU.mult), "win")
            VS.mark(eng.tensor_copy(wini[:, :], win[:, :]), "wini")
            PS.wait(eng, "last")
            VS.mark(eng.scalar_tensor_tensor(ctmp[:, :], cmask[:, :], 0.0, pG[1][0:NR, 0:NR], ALU.is_gt, ALU.mult), "ctmp")
            VS.wait(eng, "ctmp")
            VS.mark(eng.tensor_reduce(carry[:, :], ctmp[:, :], AX.X, ALU.max), "carry")
            VS.wait(eng, "carry")
            VS.mark(eng.tensor_scalar(stt[:, :], stt[:, :], carry[:, 0:1], None, ALU.max), "stt")
            VS.wait(eng, "stt")
            VS.mark(eng.tensor_tensor(stt[:, :], eid, stt[:, :], ALU.subtract), "slot")
            eng.wait_ge(s_run, 16)
            VS.wait(eng, "wini")
            VS.mark(eng.tensor_scalar(wjunk, wrun, thr[:, 0:1], 0.0, ALU.is_lt, ALU.add,
                                      accum_out=cnt2[:, :]), "cnt2")
            VS.wait(eng, "cnt2")
            VS.mark(eng.tensor_tensor(rb[:, :], rb[:, :], cnt2[:, :], ALU.add), "rb")
            PS.wait(eng, "rb")
            VS.mark(eng.tensor_copy(rbrow[:, :], pU[0:1, 0:128]), "rbrow")
            VS.mark(eng.tensor_copy(rbf[:, :], pU[0:1, 0:128]), "rbf")
            for c in range(NCH):
                a, z = c * CH, (c + 1) * CH
                eng.wait_ge(s_x[c], 48)
                for r in range(a, z):
                    last = eng.bn_stats(st6[:, r, :], X[:, r, :])
                VS.mark(last, f"bn{c}")
                VS.wait(eng, f"bn{c}")
                me, mo = st6[:, a:z, 1], st6[:, a:z, 4]
                VS.mark(eng.tensor_tensor(mean[:, a:z], me, mo, ALU.add), f"sum{c}")
                VS.mark(eng.tensor_tensor(dif[:, a:z], me, mo, ALU.subtract), f"dif{c}")
                VS.wait(eng, f"dif{c}")
                VS.mark(eng.tensor_scalar(mean[:, a:z], mean[:, a:z], 0.5, None, ALU.mult), f"mean{c}")
                VS.mark(eng.tensor_tensor(dif[:, a:z], dif[:, a:z], dif[:, a:z], ALU.mult), f"sq{c}")
                VS.mark(eng.tensor_tensor(var[:, a:z], st6[:, a:z, 2], st6[:, a:z, 5], ALU.add), f"m2{c}")
                VS.wait(eng, f"m2{c}")
                VS.mark(eng.scalar_tensor_tensor(var[:, a:z], dif[:, a:z], D / 4.0, var[:, a:z], ALU.mult, ALU.add), f"var{c}")
                AS.wait(eng, f"sq{c}")
                VS.mark(eng.reciprocal(rstd[:, a:z], rstd[:, a:z]), f"rstd{c}")
                VS.wait(eng, f"rstd{c}")
                VS.mark(eng.scalar_tensor_tensor(nmr[:, a:z], mean[:, a:z], -1.0, rstd[:, a:z], ALU.mult, ALU.mult), f"nmr{c}")

            R = slice(0, NB)

            def own(line, b, name, ins):
                line.mark(ins, b, name)
                line.wait(eng, b, name)

            def prep_meta(b):
                q = b % 3
                PA.wait(eng, b, "mT")
                VA.mark(eng.tensor_copy(idx[q][:, :], pA[:, 0:TP]), b, "idx")
                eng.tensor_scalar(dlb[q][:, :], pA[:, 32:32 + TP], boff[:, b:b + 1], None, ALU.subtract)
                eng.tensor_copy(slb[q][:, :], pA[:, 64:64 + TP])
                VA.mark(eng.tensor_copy(dec_[q][:, :], pA[:, 96:96 + TP]), b, "M")

            def prep_onehots(b):
                q = b % 2
                VA.wait(eng, b, "M")
                VB.mark(eng.tensor_tensor(D01[q][:, :, :], iotaJ[:, :, :],
                                          slb[b % 3][:, :].unsqueeze(1).to_broadcast([128, SLOT, TP]), ALU.is_equal), b, "D01")
                eng.wait_ge(s_db[q], 16 * (b // 2 + 1))
                PM.wait(eng, b - 2, "Wx1")
                VB.mark(eng.tensor_scalar(O[q][:, :], dB[q][:, :], boffp[:, b:b + 1], None, ALU.is_equal), b, "O")
                AB.wait(eng, b, "Gh")
                VB.mark(eng.tensor_tensor(Gr[R, :], pB[R, 128:256], G3[q][R, 0, :], ALU.subtract), b, "Gr")
                AM.wait(eng, b - 2, "P3")
                VB.mark(eng.tensor_tensor(OT[q][:, :, :], iotaN[:, :, :],
                                          dlb[b % 3][:, :].unsqueeze(1).to_broadcast([128, NB, TP]), ALU.is_equal), b, "OT")
                AB.wait(eng, b, "Gm")
                VB.mark(eng.tensor_tensor(G3[q][R, 2, :], Gr[R, :], G3[q][R, 1, :], ALU.subtract), b, "Gl")

            def finish(b):
                q = b % 2
                PM.wait(eng, b, "out")
                eng.wait_ge(s_xb[q], 16 * (b // 2 + 1))
                if b >= 2:
                    eng.wait_ge(s_st[q], 16 * (b // 2))
                VF.mark(eng.scalar_tensor_tensor(ob[q][R, :], pO[R, :], 0.0, xb[q][R, :], ALU.max, ALU.add), b, "fin")

            IO.wait(eng, "iotaJ")
            prep_meta(0)
            prep_meta(1)
            prep_onehots(0)
            for b in range(B):
                q = b % 2
                e = b % 3

                def sel(name, ins):
                    own(VM, b, name, ins)

                eng.wait_ge(s_er, b + 1)
                for g in range(5):
                    PG.wait(eng, b, f"Gx{g}")
                    for k in range(GG[g]):
                        t = g0[g] + k
                        last = eng.tensor_tensor_reduce(
                            out=junk[:, t * 128:(t + 1) * 128], in0=Et[e][:, t * 128:(t + 1) * 128],
                            in1=pG[g % 4][:, k * 128:(k + 1) * 128], scale=1.0, scalar=0.0,
                            op0=ALU.mult, op1=ALU.add, accum_out=s[:, t:t + 1])
                    VM.mark(last, b, f"s{g}")
                VM.wait(eng, b, "s4")
                sel("sd", eng.tensor_tensor(sd[:, :], s[:, :], dec_[e][:, :], ALU.mult))
                sel("sh", eng.tensor_copy(s3[:, 0, :], sd[:, :]))
                sel("sr", eng.tensor_tensor(sr[:, 0, :], sd[:, :], s3[:, 0, :], ALU.subtract))
                sel("sm", eng.tensor_copy(s3[:, 1, :], sr[:, 0, :]))
                VM.mark(eng.tensor_tensor(sr[:, 1, :], sr[:, 0, :], s3[:, 1, :], ALU.subtract), b, "sr2")
                VM.wait(eng, b, "sr2")
                sel("sl", eng.tensor_copy(s3[:, 2, :], sr[:, 1, :]))
                PM.wait(eng, b - 1, "Sc")
                for k in range(3):
                    last = eng.tensor_tensor(Dm[:, k * SLOT:(k + 1) * SLOT, :], D01[q][:, :, :],
                                             s3[:, k, :].unsqueeze(1).to_broadcast([128, SLOT, TP]), ALU.mult)
                VM.mark(last, b, "D")
                if b >= 1:
                    finish(b - 1)
                if b + 1 < B:
                    prep_onehots(b + 1)
                if b + 2 < B:
                    prep_meta(b + 2)

                PM.wait(eng, b, "Sc")
                sel("deg", eng.tensor_copy(DEG[R, b:b + 1], pS[R, 3 * SLOT:DC]))
                sel("pen", eng.tensor_scalar(pen[R, :], iota[R, 0:SLOT], DEG[R, b:b + 1], NEG, ALU.is_ge, ALU.mult))
                sel("Sh", eng.tensor_tensor(Sm[R, :], pS[R, 0:SLOT], pen[R, :], ALU.add))
                sel("Shm", eng.tensor_tensor(S2[R, :], pS[R, SLOT:2 * SLOT], Sm[R, :], ALU.add))
                sel("Sm", eng.tensor_tensor(Sm[R, :], pS[R, 2 * SLOT:3 * SLOT], S2[R, :], ALU.add))
                sel("m8a", eng.max(v8[R, 0:8], Sm[R, :]))
                sel("neg", eng.tensor_scalar(neg[R, :], v8[R, 0:1], -1.0, None, ALU.mult))
                sel("mr1", eng.match_replace(S2[R, :], v8[R, 0:8], Sm[R, :], TAKEN))
                sel("m8b", eng.max(v8[R, 8:16], S2[R, :]))
                sel("mr2", eng.match_replace(S3[R, :], v8[R, 8:16], S2[R, :], TAKEN))
                AM.wait(eng, b, "exp")
                sel("keep", eng.scalar_tensor_tensor(wk[R, :], S3[R, :], CUT, ex[R, :], ALU.is_lt, ALU.mult,
                                                     accum_out=den[R, :]))
                sel("rec", eng.reciprocal(rden[R, :], den[R, :]))
                sel("W", eng.tensor_scalar(W[R, :], wk[R, :], rden[R, 0:1], None, ALU.mult))
                sel("Wh", eng.tensor_copy(W3[R, 0, :], W[R, :]))
                sel("Wr", eng.tensor_tensor(Wr[R, :], W[R, :], W3[R, 0, :], ALU.subtract))
                sel("Wm", eng.tensor_copy(W3[R, 1, :], Wr[R, :]))
                VM.mark(eng.tensor_tensor(W3[R, 2, :], Wr[R, :], W3[R, 1, :], ALU.subtract), b, "Wl")
                AM.wait(eng, b - 1, "P3")
                for g in range(2):
                    t, n = w0[g], GW[g]
                    PM.wait(eng, b, f"Wx{g}")
                    sel(f"jw{g}", eng.tensor_tensor(
                        jw[:, t:t + n, :], pG[g][:, 0:n * SLOT].rearrange("p (t j) -> p t j", j=SLOT),
                        D01[q][:, :, t:t + n].rearrange("p j t -> p t j"), ALU.mult))
                    VM.mark(eng.tensor_reduce(w[:, t:t + n], jw[:, t:t + n, :], AX.X, ALU.add), b, f"w{g}")
            finish(B - 1)
            general(eng, "DVE")

        @block.scalar
        def _(eng):
            VS.wait(eng, "mr0")
            eng.wait_ge(s_ew, 16)
            AS.mark(eng.activation(dec, ewt[:, :], ACT.Exp, bias=zc[0:NR, :], scale=-1.0), "dec")
            VS.wait(eng, "rawd")
            AS.mark(eng.activation(dst16[:, :], rawd[:, 1:], ACT.Copy), "d16")
            eng.wait_ge(s_src, 16)
            AS.mark(eng.activation(srcf, srci, ACT.Copy), "srcf")
            PS.wait(eng, "A")
            AS.mark(eng.activation(A[:, :], pB[:, 0:128], ACT.Copy, scale=SCALE), "A")
            PS.wait(eng, "WmT")
            AS.mark(eng.activation(WsT[:, :], pA[:, 0:128], ACT.Copy), "WsT")
            AS.mark(eng.activation(WmT[:, :], pA[:, 128:256], ACT.Copy), "WmT")
            for c in range(NCH):
                a, z = c * CH, (c + 1) * CH
                VS.wait(eng, f"var{c}")
                AS.mark(eng.activation(rstd[:, a:z], var[:, a:z], ACT.Sqrt, bias=epsc[:, :], scale=1.0 / D), f"sq{c}")
                VS.wait(eng, f"nmr{c}")
                for r in range(a, z):
                    last = eng.activation(X[:, r, :], X[:, r, :], ACT.Relu, bias=nmr[:, r:r + 1], scale=rstd[:, r:r + 1])
                AS.mark(last, f"h{c}")

            def prep_b(b):
                q = b % 2
                PM.wait(eng, b - 2, "out")
                PB.wait(eng, b, "hT")
                AB.mark(eng.activation(hT[q][:, 0:NB], pB[:, 0:NB], ACT.Copy), b, "hT")
                PB.wait(eng, b, "G")
                PG.wait(eng, b - 2, "Gx4")
                AB.mark(eng.activation(G3[q][0:NB, 0, :], pB[0:NB, 128:256], ACT.Copy), b, "Gh")
                VB.wait(eng, b, "Gr")
                AB.mark(eng.activation(G3[q][0:NB, 1, :], Gr[0:NB, :], ACT.Copy), b, "Gm")

            prep_b(0)
            for b in range(B):
                q = b % 2
                if b + 1 < B:
                    prep_b(b + 1)
                VM.wait(eng, b, "neg")
                AM.mark(eng.activation(ex[0:NB, :], Sm[0:NB, :], ACT.Exp, bias=neg[0:NB, :]), b, "exp")
                PM.wait(eng, b - 1, "agg3")
                for g in range(4):
                    VM.wait(eng, b, "w0" if p0[g] + GP[g] <= GW[0] else "w1")
                    for t in range(p0[g], p0[g] + GP[g]):
                        last = eng.activation(P[:, t * 128:t * 128 + NB], OT[q][:, :, t], ACT.Copy, scale=w[:, t:t + 1])
                    AM.mark(last, b, f"P{g}")
                PM.wait(eng, b, "agg3")
                AM.mark(eng.activation(Us[:, 0:NB], pU[:, 0:NB], ACT.Copy), b, "U")
            general(eng, "ACT")

        @block.tensor
        def _(eng):
            VS.wait(eng, "rawd")
            VS.wait(eng, "ident")
            PS.mark(eng.matmul(pG[0][:, 0:NR], lhsT=rawd[:, 1:2].to_broadcast([NR, 128]), rhs=ident[0:NR, 0:NR],
                               start=True, stop=True), "smp")
            eng.wait_ge(s_w, 64)
            PS.mark(eng.matmul(pB[:, 0:128], lhsT=wts[:, 0, :], rhs=wts[:, 1, :], start=True, stop=True), "A")
            PS.mark(eng.transpose(pA[:, 0:128], wts[:, 2, :], ident[:, :]), "WsT")
            PS.mark(eng.transpose(pA[:, 128:256], wts[:, 3, :], ident[:, :]), "WmT")
            VS.wait(eng, "scan")
            PS.mark(eng.matmul(pG[1][0:NR, 0:NR], lhsT=stt[:, RUN - 1:RUN].to_broadcast([NR, NR]),
                               rhs=ident[0:NR, 0:NR], start=True, stop=True), "last")
            VS.wait(eng, "rb")
            PS.mark(eng.matmul(pU[0:1, 0:128], lhsT=rb[:, 0:1], rhs=ident[:, :], start=True, stop=True), "rb")

            def prep_a(b):
                q = b % 2
                eng.wait_ge(s_mr[q], 64 * (b // 2 + 1))
                VA.wait(eng, b - 1, "M")
                PA.mark(eng.transpose(pA[:, 0:128], MR[q][:, :], ident[:, :]), b, "mT")

            def prep_b(b):
                q = b % 2
                eng.wait_ge(s_hb[q], 16 * (b // 2 + 1))
                VB.wait(eng, b - 1, "Gr")
                PB.mark(eng.transpose(pB[:, 0:NB], hb[q][0:NB, :], ident[0:NB, 0:NB]), b, "hT")
                AB.wait(eng, b, "hT")
                PB.mark(eng.matmul(pB[0:NB, 128:256], lhsT=hT[q][:, 0:NB], rhs=A[:, :], start=True, stop=True), b, "G")

            def expand(b, g):
                q = b % 2
                for k in range(GG[g]):
                    t = g0[g] + k
                    for i in range(3):
                        last = eng.matmul(pG[g % 4][:, k * 128:(k + 1) * 128], lhsT=O[q][0:NB, t * 128:(t + 1) * 128],
                                          rhs=G3[q][0:NB, i, :], start=(i == 0), stop=(i == 2))
                PG.mark(last, b, f"Gx{g}")

            AS.wait(eng, "WmT")
            VS.wait(eng, "rbf")
            prep_a(0)
            prep_a(1)
            prep_b(0)
            VB.wait(eng, 0, "Gl")
            for g in (2, 3, 0, 1):
                expand(0, g)
            for b in range(B):
                q = b % 2
                VM.wait(eng, b, "s0")
                expand(b, 4)
                if b + 2 < B:
                    prep_a(b + 2)
                if b + 1 < B:
                    prep_b(b + 1)
                VM.wait(eng, b, "D")
                for t in range(T):
                    last = eng.matmul(pS[0:NB, 0:DC], lhsT=OT[q][:, :, t], rhs=Dm[:, :, t], start=(t == 0), stop=(t == T - 1))
                PM.mark(last, b, "Sc")
                if b + 1 < B:
                    VB.wait(eng, b + 1, "Gl")
                    expand(b + 1, 2)
                    expand(b + 1, 3)
                VM.wait(eng, b, "Wl")
                for g in range(2):
                    for k in range(GW[g]):
                        t = w0[g] + k
                        for i in range(3):
                            last = eng.matmul(pG[g][:, k * SLOT:(k + 1) * SLOT], lhsT=O[q][0:NB, t * 128:(t + 1) * 128],
                                              rhs=W3[0:NB, i, :], start=(i == 0), stop=(i == 2))
                    PM.mark(last, b, f"Wx{g}")
                if b + 1 < B:
                    for g in range(2):
                        VM.wait(eng, b, f"w{g}")
                        expand(b + 1, g)
                VF.wait(eng, b - 1, "fin")
                for g in range(4):
                    AM.wait(eng, b, f"P{g}")
                    for t in range(p0[g], p0[g] + GP[g]):
                        last = eng.matmul(pU[:, 0:NB], lhsT=Et[b % 3][:, t * 128:(t + 1) * 128], rhs=P[:, t * 128:t * 128 + NB],
                                          start=(t == 0), stop=(t == T - 1))
                    PM.mark(last, b, f"agg{g}")
                AM.wait(eng, b, "U")
                eng.matmul(pO[0:NB, :], lhsT=hT[q][:, 0:NB], rhs=WsT[:, :], start=True, stop=False)
                PM.mark(eng.matmul(pO[0:NB, :], lhsT=Us[:, 0:NB], rhs=WmT[:, :], start=False, stop=True), b, "out")
            general(eng, "PE")


_INS = ["x", "src", "dst", "edge_weight", "L0_gnn_W_self", "L0_gnn_W_msg", "L0_gnn_W_Q", "L0_gnn_W_K"]


def kernel(**inputs):
    import numpy as _np
    import concourse.bacc as _bacc
    from concourse import mybir as _mybir
    from concourse.bass_utils import run_bass_kernel_spmd as _run

    nc = _bacc.Bacc("TRN2", target_bir_lowering=False, num_devices=1)
    arrays, args = {}, []
    for name in _INS:
        a = _np.ascontiguousarray(inputs[name])
        arrays[f"in_{name}"] = a
        args.append(nc.dram_tensor(f"in_{name}", a.shape, _mybir.dt.from_np(a.dtype), kind="ExternalInput").ap())
    args.append(nc.dram_tensor("out_0", (12500, 128), _mybir.dt.float32, kind="ExternalOutput").ap())
    gnn_kernel(nc, *args)
    r = _run(nc, [arrays], core_ids=[0])
    return _np.asarray(r.results[0]["out_0"])
```

```python
import concourse.bass as bass
from concourse import mybir
from contextlib import ExitStack


class Line:

    def __init__(self, sem, names):
        self.sem, self.names = sem, names
        self.done = 0

    def mark(self, ins, b, name):
        at = b * len(self.names) + self.names.index(name)
        assert at == self.done, (b, name, self.done)
        self.done += 1
        ins.then_inc(self.sem, 1)

    def wait(self, eng, b, name):
        if b >= 0:
            eng.wait_ge(self.sem, b * len(self.names) + self.names.index(name) + 1)


def gnn_kernel(nc, x, src, dst, ew, w_self, w_msg, w_q, w_k, out):
    f32, i32, bf16, i16 = mybir.dt.float32, mybir.dt.int32, mybir.dt.bfloat16, mybir.dt.int16
    ALU, ACT, AX = mybir.AluOpType, mybir.ActivationFunctionType, mybir.AxisListType

    N, D, M = 12500, 128, 200000
    NB, B = 125, 100
    T, TP, SLOT = 17, 18, 48
    DC = 3 * SLOT + 1
    CAP = T * 128
    RUN = 1600
    NR = M // RUN
    MP = M + CAP
    ROWS = 98
    SCALE = 1.0 / D ** 0.5
    NEG = -3.0e38
    TAKEN = -3.4e38
    CUT = -3.2e38
    EPS = 1e-5
    GG = [4, 4, 4, 4, 1]
    GW = [9, 8]
    GP = [5, 4, 4, 4]
    LEAD = 5
    CH = 14
    NCH = ROWS // CH

    H = nc.dram_tensor("H_table", [N, D], f32, kind="Internal").ap()
    D16 = nc.dram_tensor("D16_table", [1, MP], i16, kind="Internal").ap()
    META = nc.dram_tensor("META_table", [4, MP], f32, kind="Internal").ap()

    ctx = ExitStack()
    with ctx:
        def sb(name, shape, dt=f32):
            return ctx.enter_context(nc.sbuf_tensor(name, shape, dt))

        def pb(name):
            return ctx.enter_context(nc.psum_tensor(name, [128, 512], f32))

        def sem(name):
            return ctx.enter_context(nc.semaphore(name))

        iota = sb("iota", [128, 128])
        pidx = sb("pidx", [128, 1])
        ident = sb("ident", [128, 128])
        boff = sb("boff", [128, B])
        boffp = sb("boffp", [128, B])
        iotaN = sb("iotaN", [128, NB, TP], bf16)
        iotaJ = sb("iotaJ", [128, SLOT, TP], bf16)
        thr = sb("thr", [128, 1])
        ones = sb("ones", [128, 1])
        wts = sb("wts", [128, 4, 128])
        A = sb("A", [128, 128])
        WsT = sb("WsT", [128, 128])
        WmT = sb("WmT", [128, 128])
        zc = sb("zc", [128, 1])
        epsc = sb("epsc", [128, 1])

        X = sb("X", [128, ROWS, 128])
        st6 = sb("st6", [128, ROWS, 6])
        mean = sb("mean", [128, ROWS])
        dif = sb("dif", [128, ROWS])
        var = sb("var", [128, ROWS])
        rstd = sb("rstd", [128, ROWS])
        nmr = sb("nmr", [128, ROWS])

        rawi = sb("rawi", [NR, RUN + 1], i32)
        rawd = sb("rawd", [NR, RUN + 1])
        ewt = sb("ewt", [NR, RUN])
        stt = sb("stt", [NR, RUN])
        carry = sb("carry", [NR, 1])
        cmask = sb("cmask", [NR, NR])
        ctmp = sb("ctmp", [NR, NR])
        pad = sb("pad", [4, CAP])
        pad16 = sb("pad16", [1, CAP], i16)
        dst16 = sb("dst16", [NR, RUN], i16)
        cnt1 = sb("cnt1", [128, 1])
        win = sb("win", [128, 1])
        wini = sb("wini", [128, 1], i32)
        cnt2 = sb("cnt2", [128, 1])
        rb = sb("rb", [128, 1])
        rbrow = sb("rbrow", [1, 128], i32)
        rbf = sb("rbf", [1, 128])

        MR = [sb(f"MR{q}", [128, 128]) for q in range(2)]
        dec_ = [sb(f"dec{q}", [128, TP]) for q in range(3)]
        slb = [sb(f"slb{q}", [128, TP], bf16) for q in range(3)]
        dlb = [sb(f"dlb{q}", [128, TP], bf16) for q in range(3)]
        idx = [sb(f"idx{q}", [128, TP], i32) for q in range(3)]
        dB = [sb(f"dB{q}", [128, T * 128], i16) for q in range(2)]
        hb = [sb(f"hb{q}", [128, 128]) for q in range(2)]
        xb = [sb(f"xb{q}", [128, 128]) for q in range(2)]
        hT = [sb(f"hT{q}", [128, 128]) for q in range(3)]
        G3 = [sb(f"G3{q}", [128, 3, 128], bf16) for q in range(2)]
        Gr = sb("Gr", [128, 128])
        Et = [sb(f"E{q}", [128, T * 128]) for q in range(2)] + [
            X[:, a:a + T, :].rearrange("p t d -> p (t d)") for a in (26, 26 + T)]
        P = X[:, 26 + 2 * T:26 + 3 * T, :].rearrange("p t d -> p (t d)")
        junk = X[:, 26 + 3 * T:26 + 4 * T, :].rearrange("p t d -> p (t d)")
        OT = [sb(f"OT{q}", [128, NB, TP], bf16) for q in range(3)]
        O = [sb(f"O{q}", [128, T * 128], bf16) for q in range(2)]
        D01 = [sb(f"D01{q}", [128, SLOT, TP], bf16) for q in range(3)]
        Dm = sb("Dm", [128, DC, TP], bf16)
        srct = sb("srct", [NR, RUN])
        dect = sb("dect", [NR, RUN])
        eid, neq, dec = Et[0][0:NR, 0:RUN], Et[1][0:NR, 0:RUN], dect[:, :]
        srcf = srct[:, :]
        srci = srcf.bitcast(i32)
        wrunt = sb("wrun", [128, RUN], i32)
        wjunkt = sb("wjunk", [128, RUN], bf16)
        wrun, wjunk = wrunt[:, :], wjunkt[:, :]
        s = sb("s", [128, TP])
        sd = sb("sd", [128, TP])
        s3 = sb("s3", [128, 3, TP], bf16)
        sr = sb("sr", [128, 2, TP])
        w = sb("w", [128, TP])
        jw = sb("jw", [128, T, SLOT])
        DEG = sb("DEG", [128, B])
        pen = sb("pen", [128, SLOT])
        Sm = sb("Sm", [128, SLOT])
        S2 = sb("S2", [128, SLOT])
        S3 = sb("S3", [128, SLOT])
        v8 = sb("v8", [128, 16])
        neg = sb("neg", [128, 1])
        ex = sb("ex", [128, SLOT])
        wk = sb("wk", [128, SLOT])
        den = sb("den", [128, 1])
        rden = sb("rden", [128, 1])
        W = sb("W", [128, SLOT])
        Wr = sb("Wr", [128, SLOT])
        W3 = sb("W3", [128, 3, SLOT], bf16)
        Us = sb("Us", [128, 128])
        ob = [sb(f"ob{q}", [128, 128]) for q in range(2)]

        hot = X[:, 16, 0:B]
        hrow = X[0:1, 17:21, :].rearrange("p a b -> p (a b)")
        hint = sb("hint", [1, B + 1], i32)
        bcol = sb("bcol", [128, 1])
        FM = sb("FM", [128, 4])
        fidx = sb("fidx", [128, 1], i32)
        fdl = sb("fdl", [128, 1])
        fs = sb("fs", [128, 2])
        tie = sb("tie", [128, 4])
        FE, FOT, FO, GF, DG, FW, FP, UA, EQ, KP, CU = (X[:, k, :] for k in range(11))
        C1, C2 = X[:, 12:14, :].rearrange("p a b -> p (a b)"), X[:, 14:16, :].rearrange("p a b -> p (a b)")
        FC = 16 + 128

        pA = pb("pA")
        pB = pb("pB")
        pG = [pb(f"pG{g}") for g in range(4)]
        pS = pb("pS")

        def gx(g):
            return pG[g][:, :] if g < 4 else pS[:, 256:384]

        pU = pb("pU")
        pO = pU[:, 128:256]

        s_x = [sem(f"s_x{c}") for c in range(NCH)]
        s_w = sem("s_w")
        s_dst = sem("s_dst")
        s_src = sem("s_src")
        s_ew = sem("s_ew")
        s_io = sem("s_io")
        s_v = sem("s_v")
        s_a = sem("s_a")
        s_p = sem("s_p")
        s_run = sem("s_run")
        s_ht = sem("s_ht")
        s_mt = sem("s_mt")
        s_mr = [sem(f"s_mr{q}") for q in range(2)]
        s_db = [sem(f"s_db{q}") for q in range(2)]
        s_hb = [sem(f"s_hb{q}") for q in range(2)]
        s_xb = [sem(f"s_xb{q}") for q in range(2)]
        s_st = [sem(f"s_st{q}") for q in range(2)]
        s_g = [sem(f"s_g{q}") for q in range(2)]
        s_er = sem("s_er")
        s_relay = sem("s_relay")
        s_fl = sem("s_fl")
        s_fg = sem("s_fg")
        s_tick = sem("s_tick")

        SEL = ["deg", "pen", "Sh", "Shm", "Sm", "m8a", "neg", "mr1", "m8b", "mr2", "keep", "rec", "W", "Wh", "Wr", "Wm", "Wl"]
        VM = Line(sem("VM"), [f"s{g}" for g in range(5)] + ["sd", "sh", "sr", "sm", "sr2", "sl", "D"])
        VW = Line(sem("VW"), SEL + ["jw0", "jw1", "w0", "w1"])
        VF = Line(sem("VF"), ["fin"])
        VA = Line(sem("VA"), ["idx", "M"])
        VB = Line(sem("VB"), ["D01", "Gr", "OT", "O", "Gl"])
        PG = Line(sem("PG"), ["Gx0", "Gx1", "Gx2", "Gx3", "Gx4"])
        PM = Line(sem("PM"), ["agg0", "agg1", "agg2", "agg3", "out"])
        PS_ = Line(sem("PSc"), ["Sc"])
        PW = Line(sem("PW"), ["Wx0", "Wx1"])
        PA = Line(sem("PA"), ["mT"])
        PB = Line(sem("PB"), ["hT", "G"])
        AM = Line(sem("AM"), ["exp", "P0", "P1", "P2", "P3", "U"])
        AB = Line(sem("AB"), ["hT", "Gh", "Gm"])

        g0 = [sum(GG[:g]) for g in range(5)]
        w0 = [sum(GW[:g]) for g in range(2)]
        p0 = [sum(GP[:g]) for g in range(4)]

        class Once:

            def __init__(self, sm, names):
                self.sem, self.names, self.done = sm, names, 0

            def mark(self, ins, name):
                assert self.names[self.done] == name, (name, self.names[self.done])
                self.done += 1
                ins.then_inc(self.sem, 1)

            def wait(self, eng, name):
                eng.wait_ge(self.sem, self.names.index(name) + 1)

        vn = ["zero", "ident", "mr0", "rawd", "neq", "val", "scan", "c1", "winr", "win", "wini",
              "ctmp", "carry", "stt", "slot", "cnt2", "rb", "rbrow", "rbf"]
        for c in range(NCH):
            vn += [f"{k}{c}" for k in ("bn", "sum", "dif", "mean", "sq", "m2", "var", "rstd", "nmr")]
        vn += ["zero2"]
        VS = Once(s_v, vn)
        AS = Once(s_a, ["dec", "d16", "srcf", "A", "WsT", "WmT"] + [f"{k}{c}" for c in range(NCH) for k in ("sq", "h")])
        PS = Once(s_p, ["smp", "A", "WsT", "WmT", "last", "rb"])
        IO = Once(s_io, ["iota", "pidx", "boff", "boffp", "thr", "eid", "cmask", "pad", "pad16", "iotaN", "iotaJ"])

        xr = x[0:127 * ROWS, :].rearrange("(p r) d -> p r d", r=ROWS)
        hr = H[0:127 * ROWS, :].rearrange("(p r) d -> p r d", r=ROWS)
        tail = N - ROWS
        first = 127 * ROWS - tail
        nht = sum(2 + (max(c * CH, first) < (c + 1) * CH) for c in range(NCH))
        dst2 = dst.rearrange("(p r) -> p r", r=RUN)
        src2 = src.rearrange("(p r) -> p r", r=RUN)
        ew2 = ew.rearrange("(p r) -> p r", r=RUN)
        PARTS = [(0, 112), (112, 127)]

        R_ = slice(0, NB)

        def step(engine, fn, dmas=0):
            return ("step", engine, fn, dmas)

        def repeat(kind, steps):
            return (kind, None, steps, 0)

        def fetch(e, v):
            for k in (0, 1, 3):
                last = e.dma_start(FM[:, k:k + 1], META[k, bass.ds(v["e0"], 128)].rearrange("(p a) -> p a", a=1),
                                   allow_slow_non_contiguous=True).then_inc(s_fl, 16)
            return last

        SCORES = [
            step("SP", fetch, 3),
            step("DVE", lambda e, v: (e.tensor_copy(fidx[:, :], FM[:, 0:1]),
                                      e.tensor_tensor(fdl[:, :], FM[:, 1:2], bcol[:, :], ALU.subtract))[-1]),
            step("Pool", lambda e, v: e.indirect_dma_start(
                out=FE, out_offset=None, in_=H,
                in_offset=bass.IndirectOffsetOnAxis(ap=fidx[:, 0:1], axis=0)).then_inc(s_fg, 16), 1),
            step("DVE", lambda e, v: e.tensor_scalar(FOT, iota[:, :], fdl[:, 0:1], None, ALU.is_equal)),
            step("PE", lambda e, v: e.transpose(pA[R_, 0:128], FOT[:, R_], ident[:, :])),
            step("ACT", lambda e, v: e.activation(FO[R_, :], pA[R_, 0:128], ACT.Copy)),
            step("PE", lambda e, v: e.matmul(pB[:, 0:128], lhsT=FO[R_, :], rhs=GF[R_, :], start=True, stop=True)),
            step("DVE", lambda e, v: e.tensor_tensor_reduce(out=DG, in0=FE, in1=pB[:, 0:128], scale=1.0, scalar=0.0,
                                                            op0=ALU.mult, op1=ALU.add, accum_out=fs[:, 0:1])),
            step("DVE", lambda e, v: e.tensor_tensor(fs[:, 1:2], fs[:, 0:1], FM[:, 3:4], ALU.mult)),
            step("DVE", lambda e, v: e.tensor_scalar(DG, ident[:, :], fs[:, 1:2], None, ALU.mult)),
            step("PE", lambda e, v: e.matmul(pS[R_, 0:128], lhsT=FOT[:, R_], rhs=DG, start=True, stop=True)),
            step("DVE", lambda e, v: e.tensor_scalar(EQ[R_, :], FO[R_, :], 1.0, -NEG, ALU.subtract, ALU.mult)),
            step("DVE", lambda e, v: e.tensor_tensor(C1[R_, 16:FC], pS[R_, 0:128], EQ[R_, :], ALU.add)),
        ]
        BEST = [
            step("DVE", lambda e, v: e.max(v8[R_, 0:8], C1[R_, 0:FC])),
            step("DVE", lambda e, v: e.match_replace(C2[R_, 0:FC], v8[R_, 0:8], C1[R_, 0:FC], TAKEN)),
            step("DVE", lambda e, v: e.max(v8[R_, 8:16], C2[R_, 0:FC])),
            step("DVE", lambda e, v: e.tensor_copy(C1[R_, 0:16], v8[R_, 0:16])),
        ]
        MIX = [
            step("DVE", lambda e, v: (e.tensor_scalar(EQ[R_, :], C1[R_, 16:FC], v8[R_, 15:16], None, ALU.is_equal),
                                      e.tensor_scalar(KP[R_, :], C1[R_, 16:FC], v8[R_, 15:16], None, ALU.is_gt))[-1]),
            step("DVE", lambda e, v: e.tensor_tensor_scan(CU[R_, :], EQ[R_, :], EQ[R_, :], tie[R_, 0:1], ALU.add, ALU.max)),
            step("DVE", lambda e, v: e.tensor_copy(tie[R_, 0:1], CU[R_, 127:128])),
            step("DVE", lambda e, v: e.scalar_tensor_tensor(EQ[R_, :], CU[R_, :], tie[R_, 1:2], EQ[R_, :], ALU.is_le, ALU.mult)),
            step("DVE", lambda e, v: e.tensor_tensor(KP[R_, :], KP[R_, :], EQ[R_, :], ALU.add)),
            step("ACT", lambda e, v: e.activation(FW[R_, :], C1[R_, 16:FC], ACT.Exp, bias=neg[R_, :])),
            step("DVE", lambda e, v: e.scalar_tensor_tensor(FW[R_, :], FW[R_, :], rden[R_, 0:1], KP[R_, :], ALU.mult, ALU.mult)),
            step("PE", lambda e, v: e.transpose(pB[:, R_], FW[R_, :], ident[R_, R_])),
            step("ACT", lambda e, v: e.activation(FP[:, R_], pB[:, R_], ACT.Copy)),
            step("PE", lambda e, v: e.matmul(pU[:, R_], lhsT=FE, rhs=FP[:, R_], start=True, stop=True)),
            step("DVE", lambda e, v: e.tensor_tensor(UA[:, R_], UA[:, R_], pU[:, R_], ALU.add)),
        ]
        HEAVY = [
            step("SP", lambda e, v: (e.dma_start(hb[0][R_, :], H[bass.ds(v["b"] * NB, NB), :]).then_inc(s_fl, 16),
                                     e.dma_start(xb[0][R_, :], x[bass.ds(v["b"] * NB, NB), :]).then_inc(s_fl, 16)), 2),
            step("DVE", lambda e, v: (e.memset(UA, 0.0), e.memset(C1[:, 0:16], NEG), e.memset(tie[:, 0:1], 0.0),
                                      e.tensor_copy(bcol[:, :], boff[:, bass.ds(v["b"], 1)]))[-1]),
            step("PE", lambda e, v: e.transpose(pB[:, R_], hb[0][R_, :], ident[R_, R_])),
            step("ACT", lambda e, v: e.activation(hT[0][:, R_], pB[:, R_], ACT.Copy)),
            step("PE", lambda e, v: e.matmul(pA[R_, 0:128], lhsT=hT[0][:, R_], rhs=A[:, :], start=True, stop=True)),
            step("ACT", lambda e, v: e.activation(GF[R_, :], pA[R_, 0:128], ACT.Copy)),
            repeat("edges", SCORES + BEST),
            step("DVE", lambda e, v: e.tensor_scalar(neg[R_, :], v8[R_, 0:1], -1.0, None, ALU.mult)),
            step("ACT", lambda e, v: e.activation(ex[R_, 0:16], v8[R_, 0:16], ACT.Exp, bias=neg[R_, :])),
            step("DVE", lambda e, v: e.tensor_scalar(wk[R_, 0:16], v8[R_, 0:16], v8[R_, 15:16], None, ALU.is_equal)),
            step("DVE", lambda e, v: e.tensor_reduce(tie[R_, 1:2], wk[R_, 0:16], AX.X, ALU.add)),
            step("DVE", lambda e, v: e.tensor_reduce(den[R_, :], ex[R_, 0:16], AX.X, ALU.add)),
            step("DVE", lambda e, v: e.reciprocal(rden[R_, :], den[R_, :])),
            repeat("edges", SCORES + MIX),
            step("PE", lambda e, v: (e.matmul(pO[R_, :], lhsT=hT[0][:, R_], rhs=WsT[:, :], start=True, stop=False),
                                     e.matmul(pO[R_, :], lhsT=UA[:, R_], rhs=WmT[:, :], start=False, stop=True))[-1]),
            step("DVE", lambda e, v: e.scalar_tensor_tensor(ob[0][R_, :], pO[R_, :], 0.0, xb[0][R_, :], ALU.max, ALU.add)),
            step("SP", lambda e, v: e.dma_start(out[bass.ds(v["b"] * NB, NB), :], ob[0][R_, :]).then_inc(s_fl, 16), 1),
        ]
        FLAGS = [
            step("DVE", lambda e, v: e.tensor_scalar(hot[R_, :], DEG[R_, :], float(SLOT), None, ALU.is_gt)),
            step("PE", lambda e, v: e.matmul(pS[0:1, 0:B], lhsT=ones[R_, :], rhs=hot[R_, :], start=True, stop=True)),
            step("DVE", lambda e, v: (e.tensor_scalar(hrow[:, 0:B], pS[0:1, 0:B], 0.0, None, ALU.is_gt),
                                      e.tensor_tensor(hrow[:, B:2 * B], rbf[0:1, 1:B + 1], rbf[0:1, 0:B], ALU.subtract))[-1]),
            step("DVE", lambda e, v: e.scalar_tensor_tensor(hrow[:, 2 * B:3 * B], hrow[:, B:2 * B], float(CAP),
                                                            hrow[:, 0:B], ALU.is_gt, ALU.max)),
            step("DVE", lambda e, v: e.tensor_reduce(hrow[:, 3 * B:3 * B + 1], hrow[:, 2 * B:3 * B], AX.X, ALU.add)),
            step("DVE", lambda e, v: (e.tensor_copy(hint[:, 0:B], hrow[:, 2 * B:3 * B]),
                                      e.tensor_copy(hint[:, B:B + 1], hrow[:, 3 * B:3 * B + 1]))[-1]),
        ]

        def general(eng, me):
            place, mine = eng.alloc_register(f"place_{me}"), eng.alloc_register(f"mine_{me}")
            eng.reg_mov(place, 1)
            eng.reg_mov(mine, 0)
            v = {}

            def held(sm, value):
                eng.wait_ge(sm, value)
                eng.sem_inc(s_tick, 1)

            def walk(steps):
                behind = 0
                for kind, engine, what, dmas in steps:
                    if kind == "edges":
                        eng.reg_add(place, place, behind)
                        behind = 0
                        with eng.Fori(v["r0"], v["r1"], 128) as e0:
                            v["e0"] = e0
                            walk(what)
                        continue
                    if engine == me:
                        if behind:
                            eng.reg_add(place, place, behind)
                        behind = 0
                        held(s_relay, place)
                        ins = what(eng, v)
                        if dmas > 0:
                            eng.reg_add(mine, mine, 16 * dmas)
                            held(s_fl if me == "SP" else s_fg, mine)
                            eng.sem_inc(s_relay, 1)
                        else:
                            ins.then_inc(s_relay, 1)
                    behind += 1
                if behind:
                    eng.reg_add(place, place, behind)

            walk(FLAGS)
            held(s_relay, place)
            some = eng.value_load(hint[0:1, B:B + 1], min_val=0, max_val=B)
            with eng.If(some > 0):
                with eng.Fori(0, B) as b:
                    v["b"] = b
                    this = eng.value_load(hint[0:1, bass.ds(b, 1)], min_val=0, max_val=1)
                    with eng.If(this > 0):
                        v["r0"] = eng.value_load(rbrow[0:1, bass.ds(b, 1)], min_val=0, max_val=M)
                        v["r1"] = eng.value_load(rbrow[0:1, bass.ds(b + 1, 1)], min_val=0, max_val=M)
                        walk(HEAVY)

        block = ctx.enter_context(nc.Block())

        @block.sync
        def _(eng):
            eng.dma_start(rawi[:, 1:], dst2).then_inc(s_dst, 16)
            eng.dma_start(rawi[1:NR, 0:1], dst2[0:NR - 1, RUN - 1:RUN], allow_slow_non_contiguous=True).then_inc(s_dst, 16)
            for c in range(NCH):
                a, z = c * CH, (c + 1) * CH
                for p, q in PARTS:
                    eng.dma_start(X[p:q, a:z, :], xr[p:q, a:z, :]).then_inc(s_x[c], 16)
                eng.dma_start(X[127:128, a:z, :], x[tail + a:tail + z, :].rearrange("(p r) d -> p r d", p=1)).then_inc(s_x[c], 16)
                if c == 0:
                    eng.dma_start(ewt[:, :], ew2).then_inc(s_ew, 16)
                    eng.dma_start(srci, src2).then_inc(s_src, 16)
                    for k, wt in enumerate((w_q, w_k, w_self, w_msg)):
                        eng.dma_start(wts[:, k, :], wt).then_inc(s_w, 16)

            def put(row, tile):
                eng.dma_start(META[row, 0:M].rearrange("(p r) -> p r", r=RUN), tile).then_inc(s_mt, 16)

            IO.wait(eng, "pad16")
            eng.dma_start(D16[0:1, M:MP], pad16[:, :]).then_inc(s_mt, 16)
            eng.dma_start(META[0:4, M:MP], pad[:, :]).then_inc(s_mt, 16)
            VS.wait(eng, "rawd")
            eng.dma_start(META[1, 0:M].rearrange("(p r) -> p r", r=RUN), rawd[:, 1:]).then_inc(s_mt, 16)
            AS.wait(eng, "dec")
            put(3, dec)
            AS.wait(eng, "d16")
            eng.dma_start(D16[0, 0:M].rearrange("(p r) -> p r", r=RUN), dst16[:, :]).then_inc(s_mt, 16)
            AS.wait(eng, "srcf")
            put(0, srcf)
            VS.wait(eng, "slot")
            put(2, stt[:, :])
            for c in range(NCH):
                a, z = c * CH, (c + 1) * CH
                AS.wait(eng, f"h{c}")
                for p, q in PARTS:
                    eng.dma_start(hr[p:q, a:z, :], X[p:q, a:z, :]).then_inc(s_ht, 16)
                lo = max(a, first)
                if lo < z:
                    eng.dma_start(H[tail + lo:tail + z, :].rearrange("(p r) d -> p r d", p=1), X[127:128, lo:z, :]).then_inc(s_ht, 16)

            VS.wait(eng, "rbf")
            eng.wait_ge(s_mt, 16 * 7)

            def meta(b):
                q = b % 2
                PA.wait(eng, b - 2, "mT")
                r = eng.value_load(rbrow[0:1, b:b + 1], min_val=0, max_val=M)
                for k in range(4):
                    eng.dma_start(MR[q][32 * k:32 * k + T, :],
                                  META[k, bass.ds(r, CAP)].rearrange("(t e) -> t e", e=128)).then_inc(s_mr[q], 16)

            def spread(b):
                q = b % 2
                VB.wait(eng, b - 2, "O")
                r = eng.value_load(rbrow[0:1, b:b + 1], min_val=0, max_val=M)
                eng.dma_start(dB[q][:, :], D16[0:1, bass.ds(r, CAP)].to_broadcast([128, CAP])).then_inc(s_db[q], 16)

            def load_h(b):
                q = b % 2
                PB.wait(eng, b - 2, "hT")
                eng.dma_start(hb[q][0:NB, :], H[b * NB:(b + 1) * NB, :]).then_inc(s_hb[q], 16)

            def load_x(b):
                q = b % 2
                VF.wait(eng, b - 2, "fin")
                eng.dma_start(xb[q][0:NB, :], x[b * NB:(b + 1) * NB, :]).then_inc(s_xb[q], 16)

            def store(b):
                VF.wait(eng, b, "fin")
                eng.dma_start(out[b * NB:(b + 1) * NB, :], ob[b % 2][0:NB, :]).then_inc(s_st[b % 2], 16)

            VS.wait(eng, "mr0")
            meta(0)
            spread(0)
            meta(1)
            spread(1)
            meta(2)
            meta(3)
            eng.wait_ge(s_ht, 16 * nht)
            load_h(0)
            load_h(1)
            load_h(2)
            spread(2)
            for j in range(B):
                if j + 4 < B:
                    meta(j + 4)
                if j + 3 < B:
                    load_h(j + 3)
                load_x(j)
                if j >= 2:
                    store(j - 2)
                if j + 3 < B:
                    spread(j + 3)
            store(B - 2)
            store(B - 1)
            eng.wait_ge(s_st[0], 16 * (B // 2))
            eng.wait_ge(s_st[1], 16 * (B // 2))
            eng.sem_inc(s_relay, 1)
            general(eng, "SP")

        @block.gpsimd
        def _(eng):
            small = dict(allow_small_or_imprecise_dtypes=True)
            IO.mark(eng.iota(iota[:, :], pattern=[[1, 128]], base=0, channel_multiplier=0, **small), "iota")
            IO.mark(eng.iota(pidx[:, :], pattern=[[0, 1]], base=0, channel_multiplier=1, **small), "pidx")
            IO.mark(eng.iota(boff[:, :], pattern=[[NB, B]], base=0, channel_multiplier=0, **small), "boff")
            IO.mark(eng.iota(boffp[:, :], pattern=[[NB, B]], base=0, channel_multiplier=1, **small), "boffp")
            IO.mark(eng.iota(thr[:, :], pattern=[[0, 1]], base=0, channel_multiplier=NB, **small), "thr")
            IO.mark(eng.iota(eid, pattern=[[1, RUN]], base=0, channel_multiplier=RUN, **small), "eid")
            IO.mark(eng.iota(cmask[:, :], pattern=[[-1, NR]], base=0, channel_multiplier=1, **small), "cmask")
            IO.mark(eng.iota(pad[:, :], pattern=[[0, CAP]], base=0, channel_multiplier=-1, **small), "pad")
            IO.mark(eng.iota(pad16[:, :], pattern=[[0, CAP]], base=-1, channel_multiplier=0, **small), "pad16")
            IO.mark(eng.iota(iotaN[:, :, :], pattern=[[1, NB], [0, TP]], base=0, channel_multiplier=0, **small), "iotaN")
            IO.mark(eng.iota(iotaJ[:, :, :], pattern=[[1, SLOT], [0, TP]], base=0, channel_multiplier=0, **small), "iotaJ")
            VS.wait(eng, "wini")
            eng.indirect_dma_start(out=wrun, out_offset=None, in_=dst2,
                                   in_offset=bass.IndirectOffsetOnAxis(ap=wini[:, 0:1], axis=0)).then_inc(s_run, 16)
            VS.wait(eng, "rbrow")
            VS.wait(eng, "zero")
            eng.wait_ge(s_ht, 16 * nht)

            def gather(b, t):
                q = b % 4
                return eng.indirect_dma_start(
                    out=Et[q][:, t * 128:(t + 1) * 128], out_offset=None, in_=H,
                    in_offset=bass.IndirectOffsetOnAxis(ap=idx[b % 3][:, t:t + 1], axis=0)).then_inc(s_g[b % 2], 16)

            total = [eng.alloc_register(f"total{q}") for q in range(2)]
            for q in range(2):
                eng.reg_mov(total[q], 0)

            def arrived(b):
                eng.wait_ge(s_g[b % 2], total[b % 2])
                eng.sem_inc(s_er, 1)

            for b in range(B):
                q = b % 2
                VA.wait(eng, b, "idx")
                PM.wait(eng, b - 4, "agg3")
                if b == 2:
                    VS.wait(eng, "zero2")
                r0 = eng.value_load(rbrow[0:1, b:b + 1], min_val=0, max_val=M)
                r1 = eng.value_load(rbrow[0:1, b + 1:b + 2], min_val=0, max_val=M)
                n = eng.snap(r1 - r0, min_val=0, max_val=M)
                for t in range(16):
                    gather(b, t)
                    if t == 3 and b > 0:
                        arrived(b - 1)
                eng.reg_add(total[q], total[q], 16 * 16)
                for t in range(16, T):
                    with eng.If(n > t * 128):
                        gather(b, t)
                        eng.reg_add(total[q], total[q], 16)
            arrived(B - 1)
            general(eng, "Pool")

        @block.vector
        def _(eng):
            for q in range(2):
                eng.memset(Et[q][:, 16 * 128:], 0.0)
            eng.memset(zc[:, :], 0.0)
            eng.memset(epsc[:, :], EPS)
            eng.memset(ones[:, :], 1.0)
            eng.memset(s[:, :], 0.0)
            eng.memset(Dm[:, 3 * SLOT, :], 1.0)
            VS.mark(eng.memset(rawi[0:1, 0:1], -1), "zero")
            IO.wait(eng, "pidx")
            VS.mark(eng.tensor_scalar(ident[:, :], iota[:, :], pidx[:, 0:1], None, ALU.is_equal), "ident")
            eng.memset(MR[0][:, :], 0.0)
            VS.mark(eng.memset(MR[1][:, :], 0.0), "mr0")
            eng.wait_ge(s_dst, 32)
            VS.wait(eng, "zero")
            VS.mark(eng.tensor_copy(rawd[:, :], rawi[:, :]), "rawd")
            VS.wait(eng, "rawd")
            VS.mark(eng.tensor_tensor(neq, rawd[:, 1:], rawd[:, 0:RUN], ALU.not_equal), "neq")
            VS.wait(eng, "neq")
            IO.wait(eng, "cmask")
            VS.mark(eng.tensor_tensor(neq, neq, eid, ALU.mult), "val")
            VS.wait(eng, "val")
            VS.mark(eng.tensor_tensor_scan(stt[:, :], neq, neq, 0.0, ALU.max, ALU.max), "scan")
            PS.wait(eng, "smp")
            VS.mark(eng.tensor_scalar(wjunk[:, 0:NR], pG[0][:, 0:NR], thr[:, 0:1], 0.0, ALU.is_lt, ALU.add,
                                      accum_out=cnt1[:, :]), "c1")
            VS.wait(eng, "c1")
            VS.mark(eng.tensor_scalar(win[:, :], cnt1[:, :], -1.0, 0.0, ALU.add, ALU.max), "winr")
            VS.wait(eng, "winr")
            VS.mark(eng.tensor_scalar(rb[:, :], win[:, :], float(RUN), None, ALU.mult), "win")
            VS.mark(eng.tensor_copy(wini[:, :], win[:, :]), "wini")
            PS.wait(eng, "last")
            VS.mark(eng.scalar_tensor_tensor(ctmp[:, :], cmask[:, :], 0.0, pG[1][0:NR, 0:NR], ALU.is_gt, ALU.mult), "ctmp")
            VS.wait(eng, "ctmp")
            VS.mark(eng.tensor_reduce(carry[:, :], ctmp[:, :], AX.X, ALU.max), "carry")
            VS.wait(eng, "carry")
            VS.mark(eng.tensor_scalar(stt[:, :], stt[:, :], carry[:, 0:1], None, ALU.max), "stt")
            VS.wait(eng, "stt")
            VS.mark(eng.tensor_tensor(stt[:, :], eid, stt[:, :], ALU.subtract), "slot")
            eng.wait_ge(s_run, 16)
            VS.wait(eng, "wini")
            VS.mark(eng.tensor_scalar(wjunk, wrun, thr[:, 0:1], 0.0, ALU.is_lt, ALU.add,
                                      accum_out=cnt2[:, :]), "cnt2")
            VS.wait(eng, "cnt2")
            VS.mark(eng.tensor_tensor(rb[:, :], rb[:, :], cnt2[:, :], ALU.add), "rb")
            PS.wait(eng, "rb")
            VS.mark(eng.tensor_copy(rbrow[:, :], pU[0:1, 0:128]), "rbrow")
            VS.mark(eng.tensor_copy(rbf[:, :], pU[0:1, 0:128]), "rbf")
            for c in range(NCH):
                a, z = c * CH, (c + 1) * CH
                eng.wait_ge(s_x[c], 48)
                for r in range(a, z):
                    last = eng.bn_stats(st6[:, r, :], X[:, r, :])
                VS.mark(last, f"bn{c}")
                VS.wait(eng, f"bn{c}")
                me, mo = st6[:, a:z, 1], st6[:, a:z, 4]
                VS.mark(eng.tensor_tensor(mean[:, a:z], me, mo, ALU.add), f"sum{c}")
                VS.mark(eng.tensor_tensor(dif[:, a:z], me, mo, ALU.subtract), f"dif{c}")
                VS.wait(eng, f"dif{c}")
                VS.mark(eng.tensor_scalar(mean[:, a:z], mean[:, a:z], 0.5, None, ALU.mult), f"mean{c}")
                VS.mark(eng.tensor_tensor(dif[:, a:z], dif[:, a:z], dif[:, a:z], ALU.mult), f"sq{c}")
                VS.mark(eng.tensor_tensor(var[:, a:z], st6[:, a:z, 2], st6[:, a:z, 5], ALU.add), f"m2{c}")
                VS.wait(eng, f"m2{c}")
                VS.mark(eng.scalar_tensor_tensor(var[:, a:z], dif[:, a:z], D / 4.0, var[:, a:z], ALU.mult, ALU.add), f"var{c}")
                AS.wait(eng, f"sq{c}")
                VS.mark(eng.reciprocal(rstd[:, a:z], rstd[:, a:z]), f"rstd{c}")
                VS.wait(eng, f"rstd{c}")
                VS.mark(eng.scalar_tensor_tensor(nmr[:, a:z], mean[:, a:z], -1.0, rstd[:, a:z], ALU.mult, ALU.mult), f"nmr{c}")

            R = slice(0, NB)

            def own(line, b, name, ins):
                line.mark(ins, b, name)
                line.wait(eng, b, name)

            def prep_meta(b):
                q = b % 3
                PA.wait(eng, b, "mT")
                yield VA.mark(eng.tensor_copy(idx[q][:, :], pA[:, 0:TP]), b, "idx")
                yield eng.tensor_scalar(dlb[q][:, :], pA[:, 32:32 + TP], boff[:, b:b + 1], None, ALU.subtract)
                yield eng.tensor_copy(slb[q][:, :], pA[:, 64:64 + TP])
                yield VA.mark(eng.tensor_copy(dec_[q][:, :], pA[:, 96:96 + TP]), b, "M")

            def slots_of(b):
                VA.wait(eng, b, "M")
                yield VB.mark(eng.tensor_tensor(D01[b % 3][:, :, :], iotaJ[:, :, :],
                                                slb[b % 3][:, :].unsqueeze(1).to_broadcast([128, SLOT, TP]),
                                                ALU.is_equal), b, "D01")
                AB.wait(eng, b, "Gh")
                yield VB.mark(eng.tensor_tensor(Gr[R, :], pB[R, 128:256], G3[b % 2][R, 0, :], ALU.subtract), b, "Gr")
                AM.wait(eng, b - 3, "P3")
                yield VB.mark(eng.tensor_tensor(OT[b % 3][:, :, :], iotaN[:, :, :],
                                                dlb[b % 3][:, :].unsqueeze(1).to_broadcast([128, NB, TP]),
                                                ALU.is_equal), b, "OT")

            def nodes_of(b):
                q = b % 2
                eng.wait_ge(s_db[q], 16 * (b // 2 + 1))
                PW.wait(eng, b - 2, "Wx1")
                yield VB.mark(eng.tensor_scalar(O[q][:, :], dB[q][:, :], boffp[:, b:b + 1], None, ALU.is_equal), b, "O")
                AB.wait(eng, b, "Gm")
                yield VB.mark(eng.tensor_tensor(G3[q][R, 2, :], Gr[R, :], G3[q][R, 1, :], ALU.subtract), b, "Gl")

            def finish(b):
                q = b % 2
                PM.wait(eng, b, "out")
                eng.wait_ge(s_xb[q], 16 * (b // 2 + 1))
                if b >= 2:
                    eng.wait_ge(s_st[q], 16 * (b // 2))
                yield VF.mark(eng.scalar_tensor_tensor(ob[q][R, :], pO[R, :], 0.0, xb[q][R, :], ALU.max, ALU.add), b, "fin")

            def scores(b):
                for g in range(5):
                    PG.wait(eng, b, f"Gx{g}")
                    bank = gx(g)
                    for k in range(GG[g]):
                        t = g0[g] + k
                        last = eng.tensor_tensor_reduce(
                            out=junk[:, t * 128:(t + 1) * 128], in0=Et[b % 4][:, t * 128:(t + 1) * 128],
                            in1=bank[:, k * 128:(k + 1) * 128], scale=1.0, scalar=0.0,
                            op0=ALU.mult, op1=ALU.add, accum_out=s[:, t:t + 1])
                        if k == GG[g] - 1:
                            VM.mark(last, b, f"s{g}")
                        yield

            def split_scores(b):
                e = b % 3
                VM.wait(eng, b, "s4")
                yield VM.mark(eng.tensor_tensor(sd[:, :], s[:, :], dec_[e][:, :], ALU.mult), b, "sd")
                VM.wait(eng, b, "sd")
                yield VM.mark(eng.tensor_copy(s3[:, 0, :], sd[:, :]), b, "sh")
                VM.wait(eng, b, "sh")
                yield VM.mark(eng.tensor_tensor(sr[:, 0, :], sd[:, :], s3[:, 0, :], ALU.subtract), b, "sr")
                VM.wait(eng, b, "sr")
                yield VM.mark(eng.tensor_copy(s3[:, 1, :], sr[:, 0, :]), b, "sm")
                VM.wait(eng, b, "sm")
                yield VM.mark(eng.tensor_tensor(sr[:, 1, :], sr[:, 0, :], s3[:, 1, :], ALU.subtract), b, "sr2")
                VM.wait(eng, b, "sr2")
                yield VM.mark(eng.tensor_copy(s3[:, 2, :], sr[:, 1, :]), b, "sl")

            def spread_scores(b):
                PS_.wait(eng, b - 1, "Sc")
                VM.wait(eng, b, "sl")
                for k in range(3):
                    last = eng.tensor_tensor(Dm[:, k * SLOT:(k + 1) * SLOT, :], D01[b % 3][:, :, :],
                                             s3[:, k, :].unsqueeze(1).to_broadcast([128, SLOT, TP]), ALU.mult)
                    if k == 2:
                        VM.mark(last, b, "D")
                    yield

            def choose(b):
                def sel(name, ins):
                    VW.mark(ins, b, name)

                def after(name):
                    VW.wait(eng, b, name)

                PS_.wait(eng, b, "Sc")
                yield sel("deg", eng.tensor_copy(DEG[R, b:b + 1], pS[R, 3 * SLOT:DC]))
                after("deg")
                yield sel("pen", eng.tensor_scalar(pen[R, :], iota[R, 0:SLOT], DEG[R, b:b + 1], NEG, ALU.is_ge, ALU.mult))
                after("pen")
                yield sel("Sh", eng.tensor_tensor(Sm[R, :], pS[R, 0:SLOT], pen[R, :], ALU.add))
                after("Sh")
                yield sel("Shm", eng.tensor_tensor(S2[R, :], pS[R, SLOT:2 * SLOT], Sm[R, :], ALU.add))
                after("Shm")
                yield sel("Sm", eng.tensor_tensor(Sm[R, :], pS[R, 2 * SLOT:3 * SLOT], S2[R, :], ALU.add))
                after("Sm")
                yield sel("m8a", eng.max(v8[R, 0:8], Sm[R, :]))
                after("m8a")
                yield sel("neg", eng.tensor_scalar(neg[R, :], v8[R, 0:1], -1.0, None, ALU.mult))
                yield sel("mr1", eng.match_replace(S2[R, :], v8[R, 0:8], Sm[R, :], TAKEN))
                after("mr1")
                yield sel("m8b", eng.max(v8[R, 8:16], S2[R, :]))
                after("m8b")
                yield sel("mr2", eng.match_replace(S3[R, :], v8[R, 8:16], S2[R, :], TAKEN))
                after("mr2")
                AM.wait(eng, b, "exp")
                yield sel("keep", eng.scalar_tensor_tensor(wk[R, :], S3[R, :], CUT, ex[R, :], ALU.is_lt, ALU.mult,
                                                           accum_out=den[R, :]))
                after("keep")
                yield sel("rec", eng.reciprocal(rden[R, :], den[R, :]))
                after("rec")
                yield sel("W", eng.tensor_scalar(W[R, :], wk[R, :], rden[R, 0:1], None, ALU.mult))
                after("W")
                yield sel("Wh", eng.tensor_copy(W3[R, 0, :], W[R, :]))
                after("Wh")
                yield sel("Wr", eng.tensor_tensor(Wr[R, :], W[R, :], W3[R, 0, :], ALU.subtract))
                after("Wr")
                yield sel("Wm", eng.tensor_copy(W3[R, 1, :], Wr[R, :]))
                after("Wm")
                yield sel("Wl", eng.tensor_tensor(W3[R, 2, :], Wr[R, :], W3[R, 1, :], ALU.subtract))

            def weights(b):
                AM.wait(eng, b - 1, "P3")
                for g in range(2):
                    t, n = w0[g], GW[g]
                    PW.wait(eng, b, f"Wx{g}")
                    yield VW.mark(eng.tensor_tensor(
                        jw[:, t:t + n, :], pG[g][:, 0:n * SLOT].rearrange("p (t j) -> p t j", j=SLOT),
                        D01[b % 3][:, :, t:t + n].rearrange("p j t -> p t j"), ALU.mult), b, f"jw{g}")
                for g in range(2):
                    t, n = w0[g], GW[g]
                    VW.wait(eng, b, f"jw{g}")
                    yield VW.mark(eng.tensor_reduce(w[:, t:t + n], jw[:, t:t + n, :], AX.X, ALU.add), b, f"w{g}")

            def run(*parts):
                parts = list(parts)
                while parts:
                    parts = [p for p in parts if next(p, "end") != "end"]

            def then(*parts):
                for p in parts:
                    yield from p

            def some(b, part):
                return part(b) if 0 <= b < B else iter(())

            IO.wait(eng, "iotaJ")
            run(prep_meta(0))
            run(prep_meta(1))
            run(slots_of(0))
            run(nodes_of(0))
            eng.wait_ge(s_ht, 16 * nht)
            eng.memset(Et[2][:, 16 * 128:], 0.0)
            VS.mark(eng.memset(Et[3][:, 16 * 128:], 0.0), "zero2")
            for b in range(B + 1):
                if b < B:
                    eng.wait_ge(s_er, b + 1)
                now = some(b, scores)
                for _ in range(LEAD if b < B else 0):
                    next(now)
                run(now, some(b - 1, choose))
                run(some(b - 2, finish))
                run(some(b, split_scores), then(some(b + 2, prep_meta), some(b + 1, slots_of)))
                run(some(b - 1, weights), some(b + 1, nodes_of))
                run(some(b, spread_scores))
            run(finish(B - 1))
            general(eng, "DVE")

        @block.scalar
        def _(eng):
            VS.wait(eng, "mr0")
            eng.wait_ge(s_ew, 16)
            AS.mark(eng.activation(dec, ewt[:, :], ACT.Exp, bias=zc[0:NR, :], scale=-1.0), "dec")
            VS.wait(eng, "rawd")
            AS.mark(eng.activation(dst16[:, :], rawd[:, 1:], ACT.Copy), "d16")
            eng.wait_ge(s_src, 16)
            AS.mark(eng.activation(srcf, srci, ACT.Copy), "srcf")
            PS.wait(eng, "A")
            AS.mark(eng.activation(A[:, :], pB[:, 0:128], ACT.Copy, scale=SCALE), "A")
            PS.wait(eng, "WmT")
            AS.mark(eng.activation(WsT[:, :], pA[:, 0:128], ACT.Copy), "WsT")
            AS.mark(eng.activation(WmT[:, :], pA[:, 128:256], ACT.Copy), "WmT")
            for c in range(NCH):
                a, z = c * CH, (c + 1) * CH
                VS.wait(eng, f"var{c}")
                AS.mark(eng.activation(rstd[:, a:z], var[:, a:z], ACT.Sqrt, bias=epsc[:, :], scale=1.0 / D), f"sq{c}")
                VS.wait(eng, f"nmr{c}")
                for r in range(a, z):
                    last = eng.activation(X[:, r, :], X[:, r, :], ACT.Relu, bias=nmr[:, r:r + 1], scale=rstd[:, r:r + 1])
                AS.mark(last, f"h{c}")

            def prep_b(b):
                q = b % 2
                PM.wait(eng, b - 3, "out")
                PB.wait(eng, b, "hT")
                AB.mark(eng.activation(hT[b % 3][:, 0:NB], pB[:, 0:NB], ACT.Copy), b, "hT")
                PB.wait(eng, b, "G")
                PG.wait(eng, b - 2, "Gx4")
                AB.mark(eng.activation(G3[q][0:NB, 0, :], pB[0:NB, 128:256], ACT.Copy), b, "Gh")
                VB.wait(eng, b, "Gr")
                AB.mark(eng.activation(G3[q][0:NB, 1, :], Gr[0:NB, :], ACT.Copy), b, "Gm")

            prep_b(0)
            for b in range(B + 1):
                if b >= 1:
                    VW.wait(eng, b - 1, "neg")
                    AM.mark(eng.activation(ex[0:NB, :], Sm[0:NB, :], ACT.Exp, bias=neg[0:NB, :]), b - 1, "exp")
                if b + 1 < B:
                    prep_b(b + 1)
                if b >= 1:
                    c = b - 1
                    PM.wait(eng, c - 1, "agg3")
                    for g in range(4):
                        VW.wait(eng, c, "w0" if p0[g] + GP[g] <= GW[0] else "w1")
                        for t in range(p0[g], p0[g] + GP[g]):
                            last = eng.activation(P[:, t * 128:t * 128 + NB], OT[c % 3][:, :, t], ACT.Copy, scale=w[:, t:t + 1])
                        AM.mark(last, c, f"P{g}")
                    PM.wait(eng, c, "agg3")
                    AM.mark(eng.activation(Us[:, 0:NB], pU[:, 0:NB], ACT.Copy), c, "U")
            general(eng, "ACT")

        @block.tensor
        def _(eng):
            VS.wait(eng, "rawd")
            VS.wait(eng, "ident")
            PS.mark(eng.matmul(pG[0][:, 0:NR], lhsT=rawd[:, 1:2].to_broadcast([NR, 128]), rhs=ident[0:NR, 0:NR],
                               start=True, stop=True), "smp")
            eng.wait_ge(s_w, 64)
            PS.mark(eng.matmul(pB[:, 0:128], lhsT=wts[:, 0, :], rhs=wts[:, 1, :], start=True, stop=True), "A")
            PS.mark(eng.transpose(pA[:, 0:128], wts[:, 2, :], ident[:, :]), "WsT")
            PS.mark(eng.transpose(pA[:, 128:256], wts[:, 3, :], ident[:, :]), "WmT")
            VS.wait(eng, "scan")
            PS.mark(eng.matmul(pG[1][0:NR, 0:NR], lhsT=stt[:, RUN - 1:RUN].to_broadcast([NR, NR]),
                               rhs=ident[0:NR, 0:NR], start=True, stop=True), "last")
            VS.wait(eng, "rb")
            PS.mark(eng.matmul(pU[0:1, 0:128], lhsT=rb[:, 0:1], rhs=ident[:, :], start=True, stop=True), "rb")

            def prep_a(b):
                q = b % 2
                eng.wait_ge(s_mr[q], 64 * (b // 2 + 1))
                VA.wait(eng, b - 1, "M")
                PA.mark(eng.transpose(pA[:, 0:128], MR[q][:, :], ident[:, :]), b, "mT")

            def prep_b(b):
                q = b % 2
                eng.wait_ge(s_hb[q], 16 * (b // 2 + 1))
                VB.wait(eng, b - 1, "Gr")
                PB.mark(eng.transpose(pB[:, 0:NB], hb[q][0:NB, :], ident[0:NB, 0:NB]), b, "hT")
                AB.wait(eng, b, "hT")
                PB.mark(eng.matmul(pB[0:NB, 128:256], lhsT=hT[b % 3][:, 0:NB], rhs=A[:, :], start=True, stop=True), b, "G")

            def expand(b, g):
                q = b % 2
                for k in range(GG[g]):
                    t = g0[g] + k
                    for i in range(3):
                        last = eng.matmul(gx(g)[:, k * 128:(k + 1) * 128], lhsT=O[q][0:NB, t * 128:(t + 1) * 128],
                                          rhs=G3[q][0:NB, i, :], start=(i == 0), stop=(i == 2))
                PG.mark(last, b, f"Gx{g}")

            AS.wait(eng, "WmT")
            VS.wait(eng, "rbf")
            prep_a(0)
            prep_a(1)
            prep_b(0)
            VB.wait(eng, 0, "Gl")
            for g in range(4):
                expand(0, g)
            for b in range(B + 1):
                c = b - 1
                if b < B:
                    VW.wait(eng, c, "Sm")
                    expand(b, 4)
                if b + 2 < B:
                    prep_a(b + 2)
                if b + 1 < B:
                    prep_b(b + 1)
                if c >= 0:
                    VW.wait(eng, c, "Wl")
                    if b < B:
                        VM.wait(eng, b, "s1")
                    for g in range(2):
                        for k in range(GW[g]):
                            t = w0[g] + k
                            for i in range(3):
                                last = eng.matmul(pG[g][:, k * SLOT:(k + 1) * SLOT], lhsT=O[c % 2][0:NB, t * 128:(t + 1) * 128],
                                                  rhs=W3[0:NB, i, :], start=(i == 0), stop=(i == 2))
                        PW.mark(last, c, f"Wx{g}")
                if b + 1 < B:
                    VB.wait(eng, b + 1, "Gl")
                    for g in range(4):
                        if g < 2:
                            VW.wait(eng, c, f"jw{g}")
                        VM.wait(eng, b, f"s{g}")
                        expand(b + 1, g)
                if b < B:
                    VM.wait(eng, b, "D")
                    for t in range(T):
                        last = eng.matmul(pS[0:NB, 0:DC], lhsT=OT[b % 3][:, :, t], rhs=Dm[:, :, t], start=(t == 0), stop=(t == T - 1))
                    PS_.mark(last, b, "Sc")
                if c >= 0:
                    VF.wait(eng, c - 1, "fin")
                    for g in range(4):
                        AM.wait(eng, c, f"P{g}")
                        for t in range(p0[g], p0[g] + GP[g]):
                            last = eng.matmul(pU[:, 0:NB], lhsT=Et[c % 4][:, t * 128:(t + 1) * 128], rhs=P[:, t * 128:t * 128 + NB],
                                              start=(t == 0), stop=(t == T - 1))
                        PM.mark(last, c, f"agg{g}")
                    AM.wait(eng, c, "U")
                    eng.matmul(pO[0:NB, :], lhsT=hT[c % 3][:, 0:NB], rhs=WsT[:, :], start=True, stop=False)
                    PM.mark(eng.matmul(pO[0:NB, :], lhsT=Us[:, 0:NB], rhs=WmT[:, :], start=False, stop=True), c, "out")
            general(eng, "PE")


_INS = ["x", "src", "dst", "edge_weight", "L0_gnn_W_self", "L0_gnn_W_msg", "L0_gnn_W_Q", "L0_gnn_W_K"]


def kernel(**inputs):
    import numpy as _np
    import concourse.bacc as _bacc
    from concourse import mybir as _mybir
    from concourse.bass_utils import run_bass_kernel_spmd as _run

    nc = _bacc.Bacc("TRN2", target_bir_lowering=False, num_devices=1)
    arrays, args = {}, []
    for name in _INS:
        a = _np.ascontiguousarray(inputs[name])
        arrays[f"in_{name}"] = a
        args.append(nc.dram_tensor(f"in_{name}", a.shape, _mybir.dt.from_np(a.dtype), kind="ExternalInput").ap())
    args.append(nc.dram_tensor("out_0", (12500, 128), _mybir.dt.float32, kind="ExternalOutput").ap())
    gnn_kernel(nc, *args)
    r = _run(nc, [arrays], core_ids=[0])
    return _np.asarray(r.results[0]["out_0"])
```

```python
import concourse.bass as bass
from concourse import mybir
from contextlib import ExitStack


class Line:

    def __init__(self, sem, names):
        self.sem, self.names = sem, names
        self.done = 0

    def mark(self, ins, b, name):
        at = b * len(self.names) + self.names.index(name)
        assert at == self.done, (b, name, self.done)
        self.done += 1
        ins.then_inc(self.sem, 1)

    def wait(self, eng, b, name):
        if b >= 0:
            eng.wait_ge(self.sem, b * len(self.names) + self.names.index(name) + 1)


def gnn_kernel(nc, x, src, dst, ew, w_self, w_msg, w_q, w_k, out):
    f32, i32, bf16, i16 = mybir.dt.float32, mybir.dt.int32, mybir.dt.bfloat16, mybir.dt.int16
    ALU, ACT, AX = mybir.AluOpType, mybir.ActivationFunctionType, mybir.AxisListType

    N, D, M = 12500, 128, 200000
    NB, B = 125, 100
    T, TP, SLOT = 18, 18, 48
    DC = 3 * SLOT + 1
    CAP = T * 128
    RUN = 1600
    NR = M // RUN
    MP = M + CAP
    ROWS = 98
    SCALE = 1.0 / D ** 0.5
    NEG = -3.0e38
    TAKEN = -3.4e38
    CUT = -3.2e38
    EPS = 1e-5
    GG = [4, 4, 4, 4, 2]
    GW = [9, 9]
    GP = [5, 5, 4, 4]
    LEAD = 2
    SURE = 16
    CH = [16, 16, 16, 14, 14, 12, 10]
    NCH = len(CH)
    C0 = [sum(CH[:c]) for c in range(NCH + 1)]
    RBC = 3
    CP = [4, 4, 4, 4, 4, 4, 3]

    H = nc.dram_tensor("H_table", [N, D], f32, kind="Internal").ap()
    D16 = nc.dram_tensor("D16_table", [1, MP], i16, kind="Internal").ap()
    META = nc.dram_tensor("META_table", [4, MP], f32, kind="Internal").ap()

    ctx = ExitStack()
    with ctx:
        def sb(name, shape, dt=f32):
            return ctx.enter_context(nc.sbuf_tensor(name, shape, dt))

        def pb(name):
            return ctx.enter_context(nc.psum_tensor(name, [128, 512], f32))

        def sem(name):
            return ctx.enter_context(nc.semaphore(name))

        iota = sb("iota", [128, 128])
        pidx = sb("pidx", [128, 1])
        ident = sb("ident", [128, 128])
        boff = sb("boff", [128, B])
        boffp = sb("boffp", [128, B])
        iotaN = sb("iotaN", [128, NB, TP], bf16)
        iotaJ = sb("iotaJ", [128, SLOT, TP], bf16)
        thr = sb("thr", [128, 1])
        ones = sb("ones", [128, 1])
        wts = sb("wts", [128, 4, 128])
        A = sb("A", [128, 128])
        WsT = sb("WsT", [128, 128])
        WmT = sb("WmT", [128, 128])
        zc = sb("zc", [128, 1])
        epsc = sb("epsc", [128, 1])

        X = sb("X", [128, ROWS, 128])
        st6 = sb("st6", [128, ROWS, 6])
        mean = sb("mean", [128, ROWS])
        dif = sb("dif", [128, ROWS])
        var = sb("var", [128, ROWS])
        rstd = sb("rstd", [128, ROWS])
        nmr = sb("nmr", [128, ROWS])

        rawt = sb("rawi", [128, RUN + 1], i32)
        rawi = rawt[0:NR, :]
        rawd = sb("rawd", [NR, RUN + 1])
        ewtt = sb("ewt", [128, RUN])
        ewt = ewtt[0:NR, :]
        stt = sb("stt", [NR, RUN])
        carry = sb("carry", [NR, 1])
        cmask = sb("cmask", [NR, NR])
        ctmp = sb("ctmp", [NR, NR])
        pad = sb("pad", [4, CAP])
        pad16 = sb("pad16", [1, CAP], i16)
        dst16 = sb("dst16", [NR, RUN], i16)
        cnt1 = sb("cnt1", [128, 1])
        win = sb("win", [128, 1])
        wini = sb("wini", [128, 1], i32)
        cnt2 = sb("cnt2", [128, 1])
        rb = sb("rb", [128, 1])
        rbrow = sb("rbrow", [1, 128], i32)
        rbf = sb("rbf", [1, 128])
        alrow = sb("alrow", [1, 128], i32)
        alf = sb("alf", [1, 128])
        cprow = sb("cprow", [1, 128], i32)

        MR = [sb(f"MR{q}", [128, 128]) for q in range(2)]
        dec_ = [sb(f"dec{q}", [128, TP]) for q in range(3)]
        slb = [sb(f"slb{q}", [128, TP], bf16) for q in range(3)]
        dlb = [sb(f"dlb{q}", [128, TP], bf16) for q in range(3)]
        idx = [sb(f"idx{q}", [128, TP], i32) for q in range(3)]
        dB = [a[:, 0:T * 64].bitcast(i16) for a in (rawt, ewtt)]
        hb = [sb(f"hb{q}", [128, 128]) for q in range(2)]
        xb = [sb(f"xb{q}", [128, 128]) for q in range(2)]
        hT = [sb(f"hT{q}", [128, 128]) for q in range(4)]
        G3 = [sb(f"G3{q}", [128, 3, 128], bf16) for q in range(2)]
        Gr = sb("Gr", [128, 128])
        Et = [sb(f"E{q}", [128, T * 128]) for q in range(2)] + [
            X[:, a:a + T, :].rearrange("p t d -> p (t d)") for a in (26, 26 + T)]
        P = X[:, 26 + 2 * T:26 + 3 * T, :].rearrange("p t d -> p (t d)")
        junk = X[:, 26 + 3 * T:26 + 4 * T, :].rearrange("p t d -> p (t d)")
        OT = [sb(f"OT{q}", [128, NB, TP], bf16) for q in range(3)]
        O = [sb(f"O{q}", [128, T * 128], bf16) for q in range(2)]
        D01 = [sb(f"D01{q}", [128, SLOT, TP], bf16) for q in range(3)]
        Dm = sb("Dm", [128, DC, TP], bf16)
        srct = sb("srct", [NR, RUN])
        dect = sb("dect", [NR, RUN])
        eid, neq, dec = Et[0][0:NR, 0:RUN], Et[1][0:NR, 0:RUN], dect[:, :]
        srcf = srct[:, :]
        srci = srcf.bitcast(i32)
        wrunt = sb("wrun", [128, RUN], i32)
        wjunkt = sb("wjunk", [128, RUN], bf16)
        wrun, wjunk = wrunt[:, :], wjunkt[:, :]
        s = sb("s", [128, TP])
        sd = sb("sd", [128, TP])
        s3 = sb("s3", [128, 3, TP], bf16)
        sr = sb("sr", [128, 2, TP])
        w = sb("w", [128, TP])
        jw = sb("jw", [128, T, SLOT])
        DEG = sb("DEG", [128, B])
        pen = sb("pen", [128, SLOT])
        Sm = sb("Sm", [128, SLOT])
        S2 = sb("S2", [128, SLOT])
        S3 = sb("S3", [128, SLOT])
        v8 = sb("v8", [128, 16])
        neg = sb("neg", [128, 1])
        ex = sb("ex", [128, SLOT])
        wk = sb("wk", [128, SLOT])
        den = sb("den", [128, 1])
        rden = sb("rden", [128, 1])
        W = sb("W", [128, SLOT])
        Wr = sb("Wr", [128, SLOT])
        W3 = sb("W3", [128, 3, SLOT], bf16)
        Us = sb("Us", [128, 128])
        ob = [sb(f"ob{q}", [128, 128]) for q in range(2)]

        def weighted(b):
            return P if b < B - 1 else junk

        hot = X[:, 16, 0:B]
        hrow = X[0:1, 17:21, :].rearrange("p a b -> p (a b)")
        hgap, hnone, hlost = (X[0:1, k, :] for k in (21, 22, 23))
        hint = sb("hint", [1, B + 1], i32)
        bcol = sb("bcol", [128, 1])
        FM = sb("FM", [128, 4])
        fidx = sb("fidx", [128, 1], i32)
        fdl = sb("fdl", [128, 1])
        fs = sb("fs", [128, 2])
        tie = sb("tie", [128, 4])
        FE, FOT, FO, GF, DG, FW, FP, UA, EQ, KP, CU = (X[:, k, :] for k in range(11))
        C1, C2 = X[:, 12:14, :].rearrange("p a b -> p (a b)"), X[:, 14:16, :].rearrange("p a b -> p (a b)")
        FC = 16 + 128

        pA = pb("pA")
        pB = pb("pB")
        pG = [pb(f"pG{g}") for g in range(4)]
        pS = pb("pS")

        def gx(g):
            return pG[g][:, :] if g < 4 else pB[:, 256:512]

        pU = pb("pU")
        pO = pU[:, 128:256]

        s_x = [sem(f"s_x{c}") for c in range(NCH)]
        s_w = sem("s_w")
        s_dst = sem("s_dst")
        s_src = sem("s_src")
        s_ew = sem("s_ew")
        s_io = sem("s_io")
        s_v = sem("s_v")
        s_a = sem("s_a")
        s_p = sem("s_p")
        s_run = sem("s_run")
        s_ht = sem("s_ht")
        s_mt = sem("s_mt")
        s_mr = [sem(f"s_mr{q}") for q in range(2)]
        s_db = [sem(f"s_db{q}") for q in range(2)]
        s_hb = [sem(f"s_hb{q}") for q in range(2)]
        s_xb = [sem(f"s_xb{q}") for q in range(2)]
        s_st = [sem(f"s_st{q}") for q in range(2)]
        s_g = [sem(f"s_g{q}") for q in range(2)]
        s_er = sem("s_er")
        s_relay = sem("s_relay")
        s_fl = sem("s_fl")
        s_fg = sem("s_fg")
        s_tick = sem("s_tick")

        SEL = ["deg", "pen", "Sh", "Shm", "Sm", "m8a", "neg", "mr1", "m8b", "mr2", "keep", "rec", "W", "Wh", "Wr", "Wm", "Wl"]
        VM = Line(sem("VM"), [f"s{g}" for g in range(5)] + ["sd", "sh", "sr", "sm", "sr2", "sl", "D"])
        VW = Line(sem("VW"), SEL + ["jw0", "jw1", "w0", "w1"])
        VF = Line(sem("VF"), ["fin"])
        VA = Line(sem("VA"), ["idx", "M"])
        VB = Line(sem("VB"), ["D01", "OT", "Gr", "O", "Gl"])
        PG = Line(sem("PG"), ["Gx0", "Gx1", "Gx2", "Gx3", "Gx4"])
        PM = Line(sem("PM"), ["agg0", "agg1", "agg2", "agg3", "out"])
        PC = Line(sem("PSc"), ["Sc"])
        PW = Line(sem("PW"), ["Wx0", "Wx1"])
        PA = Line(sem("PA"), ["mT"])
        PB = Line(sem("PB"), ["hT", "G"])
        LP = Line(sem("LP"), ["P2", "P3"])
        AC = Line(sem("AC"), ["cp"])
        AE = Line(sem("AX"), ["exp"])
        AU = Line(sem("AU"), ["U"])
        AM = Line(sem("AM"), ["P0", "P1", "P2", "P3"])
        AB = Line(sem("AB"), ["hT", "Gh", "Gm"])

        g0 = [sum(GG[:g]) for g in range(5)]
        w0 = [sum(GW[:g]) for g in range(2)]
        p0 = [sum(GP[:g]) for g in range(4)]

        class Once:

            def __init__(self, sm, names):
                self.sem, self.names, self.done = sm, names, 0

            def mark(self, ins, name):
                assert self.names[self.done] == name, (name, self.names[self.done])
                self.done += 1
                ins.then_inc(self.sem, 1)

            def wait(self, eng, name):
                eng.wait_ge(self.sem, self.names.index(name) + 1)

        vn = ["zero", "ident", "mr0", "rawd", "neq", "val", "scan", "c1", "winr", "win", "wini",
              "ctmp", "carry", "stt"]
        for c in range(NCH + 1):
            if c < NCH:
                vn += [f"{k}{c}" for k in ("bn", "sum", "dif", "mean", "sq", "m2", "var")]
            if c > 0:
                vn += [f"rstd{c - 1}", f"nmr{c - 1}"]
            if c == RBC:
                vn += ["cnt2", "rb"]
            if c == RBC + 1:
                vn += ["rbrow", "rbf", "al", "alf", "step", "cp"]
        vn += ["zero2"]
        VS = Once(s_v, vn)
        AS = Once(s_a, ["dec", "d16", "srcf", "A", "WsT", "WmT", "sq0"] +
                  [f"{k}{c - 1 + (k == 'sq')}" for c in range(1, NCH) for k in ("sq", "h")] + [f"h{NCH - 1}"])
        PS = Once(s_p, ["smp", "A", "WsT", "WmT", "last", "rb"])
        IO = Once(s_io, ["iota", "pidx", "boff", "boffp", "thr", "eid", "cmask", "pad", "pad16", "iotaN", "iotaJ", "slot"] +
                  [f"{k}{c}" for c in range(NCH) for k in ("n", "h")])

        xr = x[0:127 * ROWS, :].rearrange("(p r) d -> p r d", r=ROWS)
        hr = H[0:127 * ROWS, :].rearrange("(p r) d -> p r d", r=ROWS)
        tail = N - ROWS
        first = 127 * ROWS - tail
        nht = sum(2 + (max(C0[c], first) < C0[c + 1]) for c in range(NCH))
        dst2 = dst.rearrange("(p r) -> p r", r=RUN)
        src2 = src.rearrange("(p r) -> p r", r=RUN)
        ew2 = ew.rearrange("(p r) -> p r", r=RUN)
        PARTS = [(0, 112), (112, 127)]

        R_ = slice(0, NB)

        def step(engine, fn, dmas=0):
            return ("step", engine, fn, dmas)

        def repeat(kind, steps):
            return (kind, None, steps, 0)

        def fetch(e, v):
            for k in (0, 1, 3):
                last = e.dma_start(FM[:, k:k + 1], META[k, bass.ds(v["e0"], 128)].rearrange("(p a) -> p a", a=1),
                                   allow_slow_non_contiguous=True).then_inc(s_fl, 16)
            return last

        SCORES = [
            step("SP", fetch, 3),
            step("DVE", lambda e, v: (e.tensor_copy(fidx[:, :], FM[:, 0:1]),
                                      e.tensor_tensor(fdl[:, :], FM[:, 1:2], bcol[:, :], ALU.subtract))[-1]),
            step("Pool", lambda e, v: e.indirect_dma_start(
                out=FE, out_offset=None, in_=H,
                in_offset=bass.IndirectOffsetOnAxis(ap=fidx[:, 0:1], axis=0)).then_inc(s_fg, 16), 1),
            step("DVE", lambda e, v: e.tensor_scalar(FOT, iota[:, :], fdl[:, 0:1], None, ALU.is_equal)),
            step("PE", lambda e, v: e.transpose(pA[R_, 0:128], FOT[:, R_], ident[:, :])),
            step("ACT", lambda e, v: e.activation(FO[R_, :], pA[R_, 0:128], ACT.Copy)),
            step("PE", lambda e, v: e.matmul(pB[:, 0:128], lhsT=FO[R_, :], rhs=GF[R_, :], start=True, stop=True)),
            step("DVE", lambda e, v: e.tensor_tensor_reduce(out=DG, in0=FE, in1=pB[:, 0:128], scale=1.0, scalar=0.0,
                                                            op0=ALU.mult, op1=ALU.add, accum_out=fs[:, 0:1])),
            step("DVE", lambda e, v: e.tensor_tensor(fs[:, 1:2], fs[:, 0:1], FM[:, 3:4], ALU.mult)),
            step("DVE", lambda e, v: e.tensor_scalar(DG, ident[:, :], fs[:, 1:2], None, ALU.mult)),
            step("PE", lambda e, v: e.matmul(pS[R_, 0:128], lhsT=FOT[:, R_], rhs=DG, start=True, stop=True)),
            step("DVE", lambda e, v: e.tensor_scalar(EQ[R_, :], FO[R_, :], 1.0, -NEG, ALU.subtract, ALU.mult)),
            step("DVE", lambda e, v: e.tensor_tensor(C1[R_, 16:FC], pS[R_, 0:128], EQ[R_, :], ALU.add)),
        ]
        BEST = [
            step("DVE", lambda e, v: e.max(v8[R_, 0:8], C1[R_, 0:FC])),
            step("DVE", lambda e, v: e.match_replace(C2[R_, 0:FC], v8[R_, 0:8], C1[R_, 0:FC], TAKEN)),
            step("DVE", lambda e, v: e.max(v8[R_, 8:16], C2[R_, 0:FC])),
            step("DVE", lambda e, v: e.tensor_copy(C1[R_, 0:16], v8[R_, 0:16])),
        ]
        MIX = [
            step("DVE", lambda e, v: (e.scalar_tensor_tensor(EQ[R_, :], C1[R_, 16:FC], v8[R_, 15:16], FO[R_, :], ALU.is_equal, ALU.mult),
                                      e.tensor_scalar(KP[R_, :], C1[R_, 16:FC], v8[R_, 15:16], None, ALU.is_gt))[-1]),
            step("DVE", lambda e, v: e.tensor_tensor_scan(CU[R_, :], EQ[R_, :], EQ[R_, :], tie[R_, 0:1], ALU.add, ALU.max)),
            step("DVE", lambda e, v: e.tensor_copy(tie[R_, 0:1], CU[R_, 127:128])),
            step("DVE", lambda e, v: e.scalar_tensor_tensor(EQ[R_, :], CU[R_, :], tie[R_, 1:2], EQ[R_, :], ALU.is_le, ALU.mult)),
            step("DVE", lambda e, v: e.tensor_tensor(KP[R_, :], KP[R_, :], EQ[R_, :], ALU.add)),
            step("ACT", lambda e, v: e.activation(FW[R_, :], C1[R_, 16:FC], ACT.Exp, bias=neg[R_, :])),
            step("DVE", lambda e, v: e.scalar_tensor_tensor(FW[R_, :], FW[R_, :], rden[R_, 0:1], KP[R_, :], ALU.mult, ALU.mult)),
            step("PE", lambda e, v: e.transpose(pB[:, R_], FW[R_, :], ident[R_, R_])),
            step("ACT", lambda e, v: e.activation(FP[:, R_], pB[:, R_], ACT.Copy)),
            step("PE", lambda e, v: e.matmul(pU[:, R_], lhsT=FE, rhs=FP[:, R_], start=True, stop=True)),
            step("DVE", lambda e, v: e.tensor_tensor(UA[:, R_], UA[:, R_], pU[:, R_], ALU.add)),
        ]
        HEAVY = [
            step("SP", lambda e, v: (e.dma_start(hb[0][R_, :], H[bass.ds(v["b"] * NB, NB), :]).then_inc(s_fl, 16),
                                     e.dma_start(xb[0][R_, :], x[bass.ds(v["b"] * NB, NB), :]).then_inc(s_fl, 16)), 2),
            step("DVE", lambda e, v: (e.memset(UA, 0.0), e.memset(C1[:, 0:16], NEG), e.memset(tie[:, 0:1], 0.0),
                                      e.tensor_copy(bcol[:, :], boff[:, bass.ds(v["b"], 1)]))[-1]),
            step("PE", lambda e, v: e.transpose(pB[:, R_], hb[0][R_, :], ident[R_, R_])),
            step("ACT", lambda e, v: e.activation(hT[0][:, R_], pB[:, R_], ACT.Copy)),
            step("PE", lambda e, v: e.matmul(pA[R_, 0:128], lhsT=hT[0][:, R_], rhs=A[:, :], start=True, stop=True)),
            step("ACT", lambda e, v: e.activation(GF[R_, :], pA[R_, 0:128], ACT.Copy)),
            repeat("edges", SCORES + BEST),
            step("DVE", lambda e, v: e.tensor_scalar(neg[R_, :], v8[R_, 0:1], -1.0, None, ALU.mult)),
            step("ACT", lambda e, v: e.activation(ex[R_, 0:16], v8[R_, 0:16], ACT.Exp, bias=neg[R_, :])),
            step("DVE", lambda e, v: e.tensor_scalar(wk[R_, 0:16], v8[R_, 0:16], v8[R_, 15:16], None, ALU.is_equal)),
            step("DVE", lambda e, v: e.tensor_reduce(tie[R_, 1:2], wk[R_, 0:16], AX.X, ALU.add)),
            step("DVE", lambda e, v: e.tensor_reduce(den[R_, :], ex[R_, 0:16], AX.X, ALU.add)),
            step("DVE", lambda e, v: e.reciprocal(rden[R_, :], den[R_, :])),
            repeat("edges", SCORES + MIX),
            step("PE", lambda e, v: (e.matmul(pO[R_, :], lhsT=hT[0][:, R_], rhs=WsT[:, :], start=True, stop=False),
                                     e.matmul(pO[R_, :], lhsT=UA[:, R_], rhs=WmT[:, :], start=False, stop=True))[-1]),
            step("DVE", lambda e, v: e.scalar_tensor_tensor(ob[0][R_, :], pO[R_, :], 0.0, xb[0][R_, :], ALU.max, ALU.add)),
            step("SP", lambda e, v: e.dma_start(out[bass.ds(v["b"] * NB, NB), :], ob[0][R_, :]).then_inc(s_fl, 16), 1),
        ]
        FLAGS = [
            step("DVE", lambda e, v: e.tensor_scalar(hot[R_, :], DEG[R_, :], float(SLOT), None, ALU.is_gt)),
            step("PE", lambda e, v: e.matmul(pS[0:1, 0:B], lhsT=ones[R_, :], rhs=hot[R_, :], start=True, stop=True)),
            step("DVE", lambda e, v: (e.tensor_scalar(hrow[:, 0:B], pS[0:1, 0:B], 0.0, None, ALU.is_gt),
                                      e.tensor_tensor(hrow[:, B:2 * B], rbf[0:1, 1:B + 1], alf[0:1, 0:B], ALU.subtract),
                                      e.tensor_tensor(hrow[:, 2 * B:3 * B], alf[0:1, 1:B + 1], alf[0:1, 0:B], ALU.subtract))[-1]),
            step("DVE", lambda e, v: (e.tensor_scalar(hgap[:, 1:B + 1], hrow[:, 2 * B:3 * B], float((T - 1) * 128), None, ALU.is_gt),
                                      e.tensor_scalar(hnone[:, 1:B + 1], hrow[:, 2 * B:3 * B], 0.0, None, ALU.is_equal),
                                      e.memset(hgap[:, 0:1], 0.0), e.memset(hnone[:, 0:1], 0.0))[-1]),
            step("DVE", lambda e, v: e.tensor_tensor_scan(hlost[:, 0:B], hnone[:, 0:B], hgap[:, 0:B], 0.0, ALU.mult, ALU.max)),
            step("DVE", lambda e, v: e.scalar_tensor_tensor(hrow[:, 2 * B:3 * B], hrow[:, B:2 * B], float(CAP),
                                                            hrow[:, 0:B], ALU.is_gt, ALU.max)),
            step("DVE", lambda e, v: e.tensor_tensor(hrow[:, 2 * B:3 * B], hrow[:, 2 * B:3 * B], hlost[:, 0:B], ALU.max)),
            step("DVE", lambda e, v: e.tensor_reduce(hrow[:, 3 * B:3 * B + 1], hrow[:, 2 * B:3 * B], AX.X, ALU.add)),
            step("DVE", lambda e, v: (e.tensor_copy(hint[:, 0:B], hrow[:, 2 * B:3 * B]),
                                      e.tensor_copy(hint[:, B:B + 1], hrow[:, 3 * B:3 * B + 1]))[-1]),
        ]

        CLOSE = [step("SP", None)]

        def relay(eng, me):
            place, mine = eng.alloc_register(f"place_{me}"), eng.alloc_register(f"mine_{me}")
            eng.reg_mov(place, 1)
            eng.reg_mov(mine, 0)
            v = {}

            def held(sm, value):
                eng.wait_ge(sm, value)
                eng.sem_inc(s_tick, 1)

            def walk(steps):
                behind = 0
                for kind, engine, what, dmas in steps:
                    if kind == "edges":
                        eng.reg_add(place, place, behind)
                        behind = 0
                        with eng.Fori(v["r0"], v["r1"], 128) as e0:
                            v["e0"] = e0
                            walk(what)
                        continue
                    if engine == me:
                        if behind:
                            eng.reg_add(place, place, behind)
                        behind = 0
                        held(s_relay, place)
                        if what is None:
                            eng.sem_inc(s_relay, 1)
                            behind += 1
                            continue
                        ins = what(eng, v)
                        if dmas > 0:
                            eng.reg_add(mine, mine, 16 * dmas)
                            held(s_fl if me == "SP" else s_fg, mine)
                            eng.sem_inc(s_relay, 1)
                        else:
                            ins.then_inc(s_relay, 1)
                    behind += 1
                if behind:
                    eng.reg_add(place, place, behind)

            def general():
                walk(CLOSE)
                held(s_relay, place)
                some = eng.value_load(hint[0:1, B:B + 1], min_val=0, max_val=B)
                with eng.If(some > 0):
                    with eng.Fori(0, B) as b:
                        v["b"] = b
                        this = eng.value_load(hint[0:1, bass.ds(b, 1)], min_val=0, max_val=1)
                        with eng.If(this > 0):
                            v["r0"] = eng.value_load(rbrow[0:1, bass.ds(b, 1)], min_val=0, max_val=M)
                            v["r1"] = eng.value_load(rbrow[0:1, bass.ds(b + 1, 1)], min_val=0, max_val=M)
                            walk(HEAVY)

            return walk, general

        block = ctx.enter_context(nc.Block())

        @block.sync
        def _(eng):
            eng.dma_start(rawi[:, 1:], dst2).then_inc(s_dst, 16)
            eng.dma_start(rawi[1:NR, 0:1], dst2[0:NR - 1, RUN - 1:RUN], allow_slow_non_contiguous=True).then_inc(s_dst, 16)
            for c in range(NCH):
                a, z = C0[c], C0[c + 1]
                for p, q in PARTS:
                    eng.dma_start(X[p:q, a:z, :], xr[p:q, a:z, :]).then_inc(s_x[c], 16)
                eng.dma_start(X[127:128, a:z, :], x[tail + a:tail + z, :].rearrange("(p r) d -> p r d", p=1)).then_inc(s_x[c], 16)
                if c == 0:
                    eng.dma_start(ewt[:, :], ew2).then_inc(s_ew, 16)
                    eng.dma_start(srci, src2).then_inc(s_src, 16)
                    for k, wt in enumerate((w_q, w_k, w_self, w_msg)):
                        eng.dma_start(wts[:, k, :], wt).then_inc(s_w, 16)

            def put(row, tile):
                eng.dma_start(META[row, 0:M].rearrange("(p r) -> p r", r=RUN), tile).then_inc(s_mt, 16)

            VS.wait(eng, "rawd")
            eng.dma_start(META[1, 0:M].rearrange("(p r) -> p r", r=RUN), rawd[:, 1:]).then_inc(s_mt, 16)
            AS.wait(eng, "dec")
            put(3, dec)
            AS.wait(eng, "d16")
            eng.dma_start(D16[0, 0:M].rearrange("(p r) -> p r", r=RUN), dst16[:, :]).then_inc(s_mt, 16)
            AS.wait(eng, "srcf")
            put(0, srcf)
            IO.wait(eng, "pad16")
            eng.dma_start(D16[0:1, M:MP], pad16[:, :]).then_inc(s_mt, 16)
            eng.dma_start(META[0:4, M:MP], pad[:, :]).then_inc(s_mt, 16)
            IO.wait(eng, "slot")
            put(2, stt[:, :])
            def meta(b):
                q = b % 2
                PA.wait(eng, b - 2, "mT")
                r = eng.value_load(alrow[0:1, b:b + 1], min_val=0, max_val=M)
                for k in range(4):
                    eng.dma_start(MR[q][32 * k:32 * k + T, :],
                                  META[k, bass.ds(r, CAP)].rearrange("(t e) -> t e", e=128)).then_inc(s_mr[q], 16)

            def spread(b):
                q = b % 2
                VB.wait(eng, b - 2, "O")
                r = eng.value_load(alrow[0:1, b:b + 1], min_val=0, max_val=M)
                eng.dma_start(dB[q][:, :], D16[0:1, bass.ds(r, CAP)].to_broadcast([128, CAP])).then_inc(s_db[q], 16)

            def load_h(b):
                q = b % 2
                PB.wait(eng, b - 2, "hT")
                eng.dma_start(hb[q][0:NB, :], H[b * NB:(b + 1) * NB, :]).then_inc(s_hb[q], 16)

            def load_x(b):
                q = b % 2
                VF.wait(eng, b - 2, "fin")
                eng.dma_start(xb[q][0:NB, :], x[b * NB:(b + 1) * NB, :]).then_inc(s_xb[q], 16)

            def store(b):
                VF.wait(eng, b, "fin")
                eng.dma_start(out[b * NB:(b + 1) * NB, :], ob[b % 2][0:NB, :]).then_inc(s_st[b % 2], 16)

            for c in range(NCH):
                a, z = C0[c], C0[c + 1]
                AS.wait(eng, f"h{c}")
                IO.wait(eng, f"h{c}")
                for p, q in PARTS:
                    eng.dma_start(hr[p:q, a:z, :], X[p:q, a:z, :]).then_inc(s_ht, 16)
                lo = max(a, first)
                if lo < z:
                    eng.dma_start(H[tail + lo:tail + z, :].rearrange("(p r) d -> p r d", p=1), X[127:128, lo:z, :]).then_inc(s_ht, 16)
                if c == NCH - 4:
                    VS.wait(eng, "mr0")
                    VS.wait(eng, "cp")
                    eng.wait_ge(s_mt, 16 * 7)
                    meta(0)
                if c == NCH - 3:
                    meta(1)

            AS.wait(eng, "dec")
            spread(0)
            spread(1)
            meta(2)
            meta(3)
            eng.wait_ge(s_ht, 16 * nht)
            load_h(0)
            load_h(1)
            load_h(2)
            spread(2)
            for j in range(B):
                if j + 4 < B:
                    meta(j + 4)
                if j + 3 < B:
                    load_h(j + 3)
                if j + 3 < B:
                    spread(j + 3)
                load_x(j)
                if j >= 2:
                    store(j - 2)
            store(B - 2)
            store(B - 1)
            eng.wait_ge(s_st[0], 16 * (B // 2))
            eng.wait_ge(s_st[1], 16 * (B // 2))
            walk, general = relay(eng, "SP")
            walk(FLAGS)
            general()

        @block.gpsimd
        def _(eng):
            small = dict(allow_small_or_imprecise_dtypes=True)
            IO.mark(eng.iota(iota[:, :], pattern=[[1, 128]], base=0, channel_multiplier=0, **small), "iota")
            IO.mark(eng.iota(pidx[:, :], pattern=[[0, 1]], base=0, channel_multiplier=1, **small), "pidx")
            IO.mark(eng.iota(boff[:, :], pattern=[[NB, B]], base=0, channel_multiplier=0, **small), "boff")
            IO.mark(eng.iota(boffp[:, :], pattern=[[NB, B]], base=0, channel_multiplier=1, **small), "boffp")
            IO.mark(eng.iota(thr[:, :], pattern=[[0, 1]], base=0, channel_multiplier=NB, **small), "thr")
            IO.mark(eng.iota(eid, pattern=[[1, RUN]], base=0, channel_multiplier=RUN, **small), "eid")
            IO.mark(eng.iota(cmask[:, :], pattern=[[-1, NR]], base=0, channel_multiplier=1, **small), "cmask")
            VS.wait(eng, "wini")
            eng.indirect_dma_start(out=wrun, out_offset=None, in_=dst2,
                                   in_offset=bass.IndirectOffsetOnAxis(ap=wini[:, 0:1], axis=0)).then_inc(s_run, 16)
            IO.mark(eng.iota(pad[:, :], pattern=[[0, CAP]], base=0, channel_multiplier=-1, **small), "pad")
            IO.mark(eng.iota(pad16[:, :], pattern=[[0, CAP]], base=-1, channel_multiplier=0, **small), "pad16")
            IO.mark(eng.iota(iotaN[:, :, :], pattern=[[1, NB], [0, TP]], base=0, channel_multiplier=0, **small), "iotaN")
            IO.mark(eng.iota(iotaJ[:, :, :], pattern=[[1, SLOT], [0, TP]], base=0, channel_multiplier=0, **small), "iotaJ")
            VS.wait(eng, "stt")
            IO.mark(eng.tensor_tensor(stt[:, :], eid, stt[:, :], ALU.subtract), "slot")
            for c in range(NCH):
                VS.wait(eng, f"nmr{c}")
                for r in range(C0[c], C0[c] + CP[c]):
                    last = eng.tensor_scalar(X[:, r, :], X[:, r, :], rstd[:, r:r + 1], nmr[:, r:r + 1], ALU.mult, ALU.add)
                IO.mark(last, f"n{c}")
                IO.wait(eng, f"n{c}")
                rows = X[:, C0[c]:C0[c] + CP[c], :]
                IO.mark(eng.tensor_scalar(rows, rows, 0.0, None, ALU.max), f"h{c}")
            VS.wait(eng, "cp")
            VS.wait(eng, "zero")
            eng.wait_ge(s_ht, 16 * nht)

            def gather(b, t):
                q = b % 4
                return eng.indirect_dma_start(
                    out=Et[q][:, t * 128:(t + 1) * 128], out_offset=None, in_=H,
                    in_offset=bass.IndirectOffsetOnAxis(ap=idx[b % 3][:, t:t + 1], axis=0)).then_inc(s_g[b % 2], 16)

            total = [eng.alloc_register(f"total{q}") for q in range(2)]
            for q in range(2):
                eng.reg_mov(total[q], 0)

            def arrived(b):
                eng.wait_ge(s_g[b % 2], total[b % 2])
                eng.sem_inc(s_er, 1)

            for b in range(B):
                q = b % 2
                VA.wait(eng, b, "idx")
                PM.wait(eng, b - 4, "agg3")
                if b == 2:
                    VS.wait(eng, "zero2")
                AC.wait(eng, b - 4, "cp")
                r0 = eng.value_load(alrow[0:1, b:b + 1], min_val=0, max_val=M)
                r1 = eng.value_load(alrow[0:1, b + 1:b + 2], min_val=0, max_val=M)
                n = eng.snap(r1 - r0, min_val=0, max_val=M)
                for t in range(1 if b else 0, SURE):
                    gather(b, t)
                    if t == 4 and b > 0:
                        arrived(b - 1)
                eng.reg_add(total[q], total[q], 16 * (SURE - 1 if b else SURE))
                for t in range(SURE, T):
                    with eng.If(n > (t - 1) * 128):
                        gather(b, t)
                        eng.reg_add(total[q], total[q], 16)
            arrived(B - 1)
            walk, general = relay(eng, "Pool")
            walk(FLAGS)
            general()

        @block.vector
        def _(eng):
            for q in range(2):
                eng.memset(Et[q][:, 16 * 128:], 0.0)
            eng.memset(zc[:, :], 0.0)
            eng.memset(epsc[:, :], EPS)
            eng.memset(ones[:, :], 1.0)
            eng.memset(s[:, :], 0.0)
            eng.memset(Dm[:, 3 * SLOT, :], 1.0)
            VS.mark(eng.memset(rawi[0:1, 0:1], -1), "zero")
            IO.wait(eng, "pidx")
            VS.mark(eng.tensor_scalar(ident[:, :], iota[:, :], pidx[:, 0:1], None, ALU.is_equal), "ident")
            eng.memset(MR[0][:, :], 0.0)
            VS.mark(eng.memset(MR[1][:, :], 0.0), "mr0")
            eng.wait_ge(s_dst, 32)
            VS.wait(eng, "zero")
            VS.mark(eng.tensor_copy(rawd[:, :], rawi[:, :]), "rawd")
            VS.wait(eng, "rawd")
            VS.mark(eng.tensor_tensor(neq, rawd[:, 1:], rawd[:, 0:RUN], ALU.not_equal), "neq")
            VS.wait(eng, "neq")
            IO.wait(eng, "cmask")
            VS.mark(eng.tensor_tensor(neq, neq, eid, ALU.mult), "val")
            VS.wait(eng, "val")
            VS.mark(eng.tensor_tensor_scan(stt[:, :], neq, neq, 0.0, ALU.max, ALU.max), "scan")
            PS.wait(eng, "smp")
            VS.mark(eng.tensor_scalar(wjunk[:, 0:NR], pG[0][:, 0:NR], thr[:, 0:1], 0.0, ALU.is_lt, ALU.add,
                                      accum_out=cnt1[:, :]), "c1")
            VS.wait(eng, "c1")
            VS.mark(eng.tensor_scalar(win[:, :], cnt1[:, :], -1.0, 0.0, ALU.add, ALU.max), "winr")
            VS.wait(eng, "winr")
            VS.mark(eng.tensor_scalar(rb[:, :], win[:, :], float(RUN), None, ALU.mult), "win")
            VS.mark(eng.tensor_copy(wini[:, :], win[:, :]), "wini")
            PS.wait(eng, "last")
            VS.mark(eng.scalar_tensor_tensor(ctmp[:, :], cmask[:, :], 0.0, pG[1][0:NR, 0:NR], ALU.is_gt, ALU.mult), "ctmp")
            VS.wait(eng, "ctmp")
            VS.mark(eng.tensor_reduce(carry[:, :], ctmp[:, :], AX.X, ALU.max), "carry")
            VS.wait(eng, "carry")
            VS.mark(eng.tensor_scalar(stt[:, :], stt[:, :], carry[:, 0:1], None, ALU.max), "stt")
            def stats(c):
                a, z = C0[c], C0[c + 1]
                eng.wait_ge(s_x[c], 48)
                for r in range(a, z):
                    last = eng.bn_stats(st6[:, r, :], X[:, r, :])
                VS.mark(last, f"bn{c}")
                VS.wait(eng, f"bn{c}")
                me, mo = st6[:, a:z, 1], st6[:, a:z, 4]
                VS.mark(eng.tensor_tensor(mean[:, a:z], me, mo, ALU.add), f"sum{c}")
                VS.mark(eng.tensor_tensor(dif[:, a:z], me, mo, ALU.subtract), f"dif{c}")
                VS.wait(eng, f"dif{c}")
                VS.mark(eng.tensor_scalar(mean[:, a:z], mean[:, a:z], 0.5, None, ALU.mult), f"mean{c}")
                VS.mark(eng.tensor_tensor(dif[:, a:z], dif[:, a:z], dif[:, a:z], ALU.mult), f"sq{c}")
                VS.mark(eng.tensor_tensor(var[:, a:z], st6[:, a:z, 2], st6[:, a:z, 5], ALU.add), f"m2{c}")
                VS.wait(eng, f"m2{c}")
                VS.mark(eng.scalar_tensor_tensor(var[:, a:z], dif[:, a:z], D / 4.0, var[:, a:z], ALU.mult, ALU.add), f"var{c}")

            def norms(c):
                a, z = C0[c], C0[c + 1]
                AS.wait(eng, f"sq{c}")
                VS.mark(eng.reciprocal(rstd[:, a:z], rstd[:, a:z]), f"rstd{c}")
                VS.wait(eng, f"rstd{c}")
                VS.mark(eng.scalar_tensor_tensor(nmr[:, a:z], mean[:, a:z], -1.0, rstd[:, a:z], ALU.mult, ALU.mult), f"nmr{c}")

            for c in range(NCH + 1):
                if c < NCH:
                    stats(c)
                if c > 0:
                    norms(c - 1)
                if c == RBC:
                    eng.wait_ge(s_run, 16)
                    VS.wait(eng, "wini")
                    VS.mark(eng.tensor_scalar(wjunk, wrun, thr[:, 0:1], 0.0, ALU.is_lt, ALU.add,
                                              accum_out=cnt2[:, :]), "cnt2")
                    VS.wait(eng, "cnt2")
                    VS.mark(eng.tensor_tensor(rb[:, :], rb[:, :], cnt2[:, :], ALU.add), "rb")
                if c == RBC + 1:
                    PS.wait(eng, "rb")
                    VS.mark(eng.tensor_copy(rbrow[:, :], pU[0:1, 0:128]), "rbrow")
                    VS.mark(eng.tensor_copy(rbf[:, :], pU[0:1, 0:128]), "rbf")
                    VS.wait(eng, "rbrow")
                    VS.mark(eng.tensor_scalar(alrow[:, :], rbrow[:, :], -128, None, ALU.bitwise_and), "al")
                    VS.wait(eng, "al")
                    VS.mark(eng.tensor_copy(alf[:, :], alrow[:, :]), "alf")
                    VS.mark(eng.tensor_tensor(cprow[:, 1:B + 1], alrow[:, 1:B + 1], alrow[:, 0:B], ALU.subtract), "step")
                    VS.wait(eng, "step")
                    VS.mark(eng.tensor_scalar(cprow[:, 1:B + 1], cprow[:, 1:B + 1], (T - 1) * 128, None, ALU.min), "cp")

            R = slice(0, NB)

            def prep_meta(b):
                q = b % 3
                PA.wait(eng, b, "mT")
                yield VA.mark(eng.tensor_copy(idx[q][:, :], pA[:, 0:TP]), b, "idx")
                yield eng.tensor_scalar(dlb[q][:, :], pA[:, 32:32 + TP], boff[:, b:b + 1], None, ALU.subtract)
                yield eng.tensor_copy(slb[q][:, :], pA[:, 64:64 + TP])
                yield VA.mark(eng.tensor_copy(dec_[q][:, :], pA[:, 96:96 + TP]), b, "M")

            def slots_of(b):
                VA.wait(eng, b, "M")
                yield VB.mark(eng.tensor_tensor(D01[b % 3][:, :, :], iotaJ[:, :, :],
                                                slb[b % 3][:, :].unsqueeze(1).to_broadcast([128, SLOT, TP]),
                                                ALU.is_equal), b, "D01")
                AM.wait(eng, b - 3, "P3")
                yield VB.mark(eng.tensor_tensor(OT[b % 3][:, :, :], iotaN[:, :, :],
                                                dlb[b % 3][:, :].unsqueeze(1).to_broadcast([128, NB, TP]),
                                                ALU.is_equal), b, "OT")
                AB.wait(eng, b, "Gh")
                yield VB.mark(eng.tensor_tensor(Gr[R, :], pB[R, 128:256], G3[b % 2][R, 0, :], ALU.subtract), b, "Gr")

            def nodes_of(b):
                q = b % 2
                eng.wait_ge(s_db[q], 16 * (b // 2 + 1))
                PW.wait(eng, b - 2, "Wx1")
                yield VB.mark(eng.tensor_scalar(O[q][:, :], dB[q][:, :], boffp[:, b:b + 1], None, ALU.is_equal), b, "O")
                AB.wait(eng, b, "Gm")
                yield VB.mark(eng.tensor_tensor(G3[q][R, 2, :], Gr[R, :], G3[q][R, 1, :], ALU.subtract), b, "Gl")

            def finish(b):
                q = b % 2
                PM.wait(eng, b, "out")
                eng.wait_ge(s_xb[q], 16 * (b // 2 + 1))
                if b >= 2:
                    eng.wait_ge(s_st[q], 16 * (b // 2))
                yield VF.mark(eng.scalar_tensor_tensor(ob[q][R, :], pO[R, :], 0.0, xb[q][R, :], ALU.max, ALU.add), b, "fin")

            def scores(b):
                for g in range(5):
                    PG.wait(eng, b, f"Gx{g}")
                    bank = gx(g)
                    for k in range(GG[g]):
                        t = g0[g] + k
                        last = eng.tensor_tensor_reduce(
                            out=junk[:, t * 128:(t + 1) * 128], in0=Et[b % 4][:, t * 128:(t + 1) * 128],
                            in1=bank[:, k * 128:(k + 1) * 128], scale=1.0, scalar=0.0,
                            op0=ALU.mult, op1=ALU.add, accum_out=s[:, t:t + 1])
                        if k == GG[g] - 1:
                            VM.mark(last, b, f"s{g}")
                        yield

            def split_scores(b):
                e = b % 3
                VM.wait(eng, b, "s4")
                yield VM.mark(eng.tensor_tensor(sd[:, :], s[:, :], dec_[e][:, :], ALU.mult), b, "sd")
                VM.wait(eng, b, "sd")
                yield VM.mark(eng.tensor_copy(s3[:, 0, :], sd[:, :]), b, "sh")
                VM.wait(eng, b, "sh")
                yield VM.mark(eng.tensor_tensor(sr[:, 0, :], sd[:, :], s3[:, 0, :], ALU.subtract), b, "sr")
                VM.wait(eng, b, "sr")
                yield VM.mark(eng.tensor_copy(s3[:, 1, :], sr[:, 0, :]), b, "sm")
                VM.wait(eng, b, "sm")
                yield VM.mark(eng.tensor_tensor(sr[:, 1, :], sr[:, 0, :], s3[:, 1, :], ALU.subtract), b, "sr2")
                VM.wait(eng, b, "sr2")
                yield VM.mark(eng.tensor_copy(s3[:, 2, :], sr[:, 1, :]), b, "sl")

            def spread_scores(b):
                PC.wait(eng, b - 1, "Sc")
                VM.wait(eng, b, "sl")
                for k in range(3):
                    last = eng.tensor_tensor(Dm[:, k * SLOT:(k + 1) * SLOT, :], D01[b % 3][:, :, :],
                                             s3[:, k, :].unsqueeze(1).to_broadcast([128, SLOT, TP]), ALU.mult)
                    if k == 2:
                        VM.mark(last, b, "D")
                    yield

            def choose(b):
                def sel(name, ins):
                    VW.mark(ins, b, name)

                def after(name):
                    VW.wait(eng, b, name)

                PC.wait(eng, b, "Sc")
                yield sel("deg", eng.tensor_copy(DEG[R, b:b + 1], pS[R, 3 * SLOT:DC]))
                after("deg")
                yield sel("pen", eng.tensor_scalar(pen[R, :], iota[R, 0:SLOT], DEG[R, b:b + 1], NEG, ALU.is_ge, ALU.mult))
                after("pen")
                yield sel("Sh", eng.tensor_tensor(Sm[R, :], pS[R, 0:SLOT], pen[R, :], ALU.add))
                after("Sh")
                yield sel("Shm", eng.tensor_tensor(S2[R, :], pS[R, SLOT:2 * SLOT], Sm[R, :], ALU.add))
                after("Shm")
                yield sel("Sm", eng.tensor_tensor(Sm[R, :], pS[R, 2 * SLOT:3 * SLOT], S2[R, :], ALU.add))
                after("Sm")
                yield sel("m8a", eng.max(v8[R, 0:8], Sm[R, :]))
                after("m8a")
                yield sel("neg", eng.tensor_scalar(neg[R, :], v8[R, 0:1], -1.0, None, ALU.mult))
                yield sel("mr1", eng.match_replace(S2[R, :], v8[R, 0:8], Sm[R, :], TAKEN))
                after("mr1")
                yield sel("m8b", eng.max(v8[R, 8:16], S2[R, :]))
                after("m8b")
                yield sel("mr2", eng.match_replace(S3[R, :], v8[R, 8:16], S2[R, :], TAKEN))
                after("mr2")
                AE.wait(eng, b, "exp")
                yield sel("keep", eng.scalar_tensor_tensor(wk[R, :], S3[R, :], CUT, ex[R, :], ALU.is_lt, ALU.mult,
                                                           accum_out=den[R, :]))
                after("keep")
                yield sel("rec", eng.reciprocal(rden[R, :], den[R, :]))
                after("rec")
                yield sel("W", eng.tensor_scalar(W[R, :], wk[R, :], rden[R, 0:1], None, ALU.mult))
                after("W")
                yield sel("Wh", eng.tensor_copy(W3[R, 0, :], W[R, :]))
                after("Wh")
                yield sel("Wr", eng.tensor_tensor(Wr[R, :], W[R, :], W3[R, 0, :], ALU.subtract))
                after("Wr")
                yield sel("Wm", eng.tensor_copy(W3[R, 1, :], Wr[R, :]))
                after("Wm")
                yield sel("Wl", eng.tensor_tensor(W3[R, 2, :], Wr[R, :], W3[R, 1, :], ALU.subtract))

            def weights(b):
                AM.wait(eng, b - 1, "P3")
                for g in range(2):
                    t, n = w0[g], GW[g]
                    PW.wait(eng, b, f"Wx{g}")
                    yield VW.mark(eng.tensor_tensor(
                        jw[:, t:t + n, :], pG[g][:, 0:n * SLOT].rearrange("p (t j) -> p t j", j=SLOT),
                        D01[b % 3][:, :, t:t + n].rearrange("p j t -> p t j"), ALU.mult), b, f"jw{g}")
                for g in range(2):
                    t, n = w0[g], GW[g]
                    VW.wait(eng, b, f"jw{g}")
                    yield VW.mark(eng.tensor_reduce(w[:, t:t + n], jw[:, t:t + n, :], AX.X, ALU.add), b, f"w{g}")

            def run(*parts):
                parts = list(parts)
                while parts:
                    parts = [p for p in parts if next(p, "end") != "end"]

            def then(*parts):
                for p in parts:
                    yield from p

            def some(b, part):
                return part(b) if 0 <= b < B else iter(())

            IO.wait(eng, "iotaJ")
            run(prep_meta(0))
            run(prep_meta(1))
            run(slots_of(0))
            run(nodes_of(0))
            eng.wait_ge(s_ht, 16 * nht)
            eng.memset(Et[2][:, 16 * 128:], 0.0)
            VS.mark(eng.memset(Et[3][:, 16 * 128:], 0.0), "zero2")
            walk, general = relay(eng, "DVE")
            for b in range(B + 2):
                picks = some(b - 1, choose)
                for _ in range(8 if b == B - 1 else 0):
                    next(picks)
                if b < B:
                    eng.wait_ge(s_er, b + 1)
                    AC.wait(eng, b - 1, "cp")
                now = some(b, scores)
                for _ in range(LEAD if b < B else 0):
                    next(now)
                run(then(now, some(b, split_scores)), picks, some(b + 2, prep_meta))
                slots = some(b + 1, slots_of)
                next(slots, None)
                run(some(b, spread_scores))
                run(slots)
                run(some(b + 1, nodes_of))
                run(some(b - 1, weights))
                if b == B:
                    eng.sem_inc(s_relay, 1)
                    walk(FLAGS[:1])
                    c = b - 1
                    VW.wait(eng, c, "w1")
                    for g in (2, 3):
                        for t in range(p0[g], p0[g] + GP[g]):
                            last = eng.tensor_scalar(weighted(c)[:, t * 128:t * 128 + NB], OT[c % 3][:, :, t], w[:, t:t + 1], None, ALU.mult)
                        LP.mark(last, 0, f"P{g}")
                    run(some(b - 2, finish))
                    walk(FLAGS[1:])
                else:
                    run(some(b - 2, finish))
            general()

        @block.scalar
        def _(eng):
            VS.wait(eng, "mr0")
            eng.wait_ge(s_ew, 16)
            AS.mark(eng.activation(dec, ewt[:, :], ACT.Exp, bias=zc[0:NR, :], scale=-1.0), "dec")
            VS.wait(eng, "rawd")
            AS.mark(eng.activation(dst16[:, :], rawd[:, 1:], ACT.Copy), "d16")
            eng.wait_ge(s_src, 16)
            AS.mark(eng.activation(srcf, srci, ACT.Copy), "srcf")
            PS.wait(eng, "A")
            AS.mark(eng.activation(A[:, :], pB[:, 0:128], ACT.Copy, scale=SCALE), "A")
            PS.wait(eng, "WmT")
            AS.mark(eng.activation(WsT[:, :], pA[:, 0:128], ACT.Copy), "WsT")
            AS.mark(eng.activation(WmT[:, :], pA[:, 128:256], ACT.Copy), "WmT")
            for c in range(NCH + 1):
                if c < NCH:
                    a, z = C0[c], C0[c + 1]
                    VS.wait(eng, f"var{c}")
                    AS.mark(eng.activation(rstd[:, a:z], var[:, a:z], ACT.Sqrt, bias=epsc[:, :], scale=1.0 / D), f"sq{c}")
                if c > 0:
                    VS.wait(eng, f"nmr{c - 1}")
                    for r in range(C0[c - 1] + CP[c - 1], C0[c]):
                        last = eng.activation(X[:, r, :], X[:, r, :], ACT.Relu, bias=nmr[:, r:r + 1], scale=rstd[:, r:r + 1])
                    AS.mark(last, f"h{c - 1}")

            def turn(b):
                PM.wait(eng, b - 4, "out")
                PB.wait(eng, b, "hT")
                AB.mark(eng.activation(hT[b % 4][:, 0:NB], pB[:, 0:NB], ACT.Copy), b, "hT")

            def split(b):
                q = b % 2
                PB.wait(eng, b, "G")
                PG.wait(eng, b - 2, "Gx4")
                AB.mark(eng.activation(G3[q][0:NB, 0, :], pB[0:NB, 128:256], ACT.Copy), b, "Gh")
                VB.wait(eng, b, "Gr")
                AB.mark(eng.activation(G3[q][0:NB, 1, :], Gr[0:NB, :], ACT.Copy), b, "Gm")

            def share(b):
                eng.wait_ge(s_er, b)
                PM.wait(eng, b - 4, "agg3")
                at = eng.value_load(cprow[0:1, b:b + 1], min_val=0, max_val=(T - 1) * 128)
                AC.mark(eng.activation(Et[b % 4][:, 0:128], Et[(b - 1) % 4][:, bass.ds(at, 128)], ACT.Copy), b - 1, "cp")

            VS.wait(eng, "cp")
            def mixed(b):
                PM.wait(eng, b, "agg3")
                AU.mark(eng.activation(Us[:, 0:NB], pU[:, 0:NB], ACT.Copy), b, "U")

            def best(b):
                VW.wait(eng, b, "neg")
                AE.mark(eng.activation(ex[0:NB, :], Sm[0:NB, :], ACT.Exp, bias=neg[0:NB, :]), b, "exp")

            turn(0)
            split(0)
            for b in range(B + 2):
                if 0 <= b - 1 < B - 1:
                    best(b - 1)
                if b + 1 < B:
                    turn(b + 1)
                if b >= 2 and b != B:
                    mixed(b - 2)
                if b + 1 < B:
                    split(b + 1)
                    share(b + 1)
                c = b - 1
                if 0 <= c < B:
                    if c < B - 1:
                        PM.wait(eng, c - 1, "agg3")
                    for g in range(4 if c < B - 1 else 2):
                        VW.wait(eng, c, "w0" if p0[g] + GP[g] <= GW[0] else "w1")
                        for t in range(p0[g], p0[g] + GP[g]):
                            last = eng.activation(weighted(c)[:, t * 128:t * 128 + NB], OT[c % 3][:, :, t], ACT.Copy, scale=w[:, t:t + 1])
                        AM.mark(last, c, f"P{g}")
                        if c == B - 2 and g == 0:
                            best(B - 1)
                        if c == B - 1 and g == 0:
                            mixed(B - 2)
            walk, general = relay(eng, "ACT")
            walk(FLAGS)
            general()

        @block.tensor
        def _(eng):
            VS.wait(eng, "rawd")
            VS.wait(eng, "ident")
            PS.mark(eng.matmul(pG[0][:, 0:NR], lhsT=rawd[:, 1:2].to_broadcast([NR, 128]), rhs=ident[0:NR, 0:NR],
                               start=True, stop=True), "smp")
            eng.wait_ge(s_w, 64)
            PS.mark(eng.matmul(pB[:, 0:128], lhsT=wts[:, 0, :], rhs=wts[:, 1, :], start=True, stop=True), "A")
            PS.mark(eng.transpose(pA[:, 0:128], wts[:, 2, :], ident[:, :]), "WsT")
            PS.mark(eng.transpose(pA[:, 128:256], wts[:, 3, :], ident[:, :]), "WmT")
            VS.wait(eng, "scan")
            PS.mark(eng.matmul(pG[1][0:NR, 0:NR], lhsT=stt[:, RUN - 1:RUN].to_broadcast([NR, NR]),
                               rhs=ident[0:NR, 0:NR], start=True, stop=True), "last")
            VS.wait(eng, "rb")
            PS.mark(eng.matmul(pU[0:1, 0:128], lhsT=rb[:, 0:1], rhs=ident[:, :], start=True, stop=True), "rb")

            def prep_a(b):
                q = b % 2
                eng.wait_ge(s_mr[q], 64 * (b // 2 + 1))
                VA.wait(eng, b - 1, "M")
                PA.mark(eng.transpose(pA[:, 0:128], MR[q][:, :], ident[:, :]), b, "mT")

            def turn(b):
                q = b % 2
                eng.wait_ge(s_hb[q], 16 * (b // 2 + 1))
                VM.wait(eng, b - 1, "s4")
                PB.mark(eng.transpose(pB[:, 0:NB], hb[q][0:NB, :], ident[0:NB, 0:NB]), b, "hT")

            def project(b):
                AB.wait(eng, b, "hT")
                PB.mark(eng.matmul(pB[0:NB, 128:256], lhsT=hT[b % 4][:, 0:NB], rhs=A[:, :], start=True, stop=True), b, "G")

            def expand(b, g):
                q = b % 2
                for k in range(GG[g]):
                    t = g0[g] + k
                    for i in range(3):
                        last = eng.matmul(gx(g)[:, k * 128:(k + 1) * 128], lhsT=O[q][0:NB, t * 128:(t + 1) * 128],
                                          rhs=G3[q][0:NB, i, :], start=(i == 0), stop=(i == 2))
                PG.mark(last, b, f"Gx{g}")

            AS.wait(eng, "WmT")
            VS.wait(eng, "rbf")
            prep_a(0)
            prep_a(1)
            turn(0)
            project(0)
            VB.wait(eng, 0, "Gl")
            for g in range(5):
                expand(0, g)
            def gather_weights(b):
                VW.wait(eng, b, "Wl")
                VM.wait(eng, min(b + 1, B - 1), "s1")
                for g in range(2):
                    for k in range(GW[g]):
                        t = w0[g] + k
                        for i in range(3):
                            last = eng.matmul(pG[g][:, k * SLOT:(k + 1) * SLOT], lhsT=O[b % 2][0:NB, t * 128:(t + 1) * 128],
                                              rhs=W3[0:NB, i, :], start=(i == 0), stop=(i == 2))
                    PW.mark(last, b, f"Wx{g}")

            walk, general = relay(eng, "PE")
            for b in range(B + 2):
                c, d = b - 1, b - 2
                if b + 2 < B:
                    prep_a(b + 2)
                if b == B:
                    gather_weights(B - 1)
                if d == B - 1:
                    walk(FLAGS)
                if d >= 0:
                    VF.wait(eng, d - 1, "fin")
                    for g in range(4):
                        if d < B - 1 or g < 2:
                            AM.wait(eng, d, f"P{g}")
                        else:
                            LP.wait(eng, 0, f"P{g}")
                        for t in range(p0[g], p0[g] + GP[g]):
                            last = eng.matmul(pU[:, 0:NB], lhsT=Et[d % 4][:, t * 128:(t + 1) * 128], rhs=weighted(d)[:, t * 128:t * 128 + NB],
                                              start=(t == 0), stop=(t == T - 1))
                        PM.mark(last, d, f"agg{g}")
                if b + 1 < B:
                    turn(b + 1)
                    project(b + 1)
                if 0 <= c < B - 1:
                    gather_weights(c)
                if d >= 0:
                    AU.wait(eng, d, "U")
                    eng.matmul(pO[0:NB, :], lhsT=hT[d % 4][:, 0:NB], rhs=WsT[:, :], start=True, stop=False)
                    PM.mark(eng.matmul(pO[0:NB, :], lhsT=Us[:, 0:NB], rhs=WmT[:, :], start=False, stop=True), d, "out")
                if b < B:
                    VM.wait(eng, b, "D")
                    for t in range(T):
                        last = eng.matmul(pS[0:NB, 0:DC], lhsT=OT[b % 3][:, :, t], rhs=Dm[:, :, t], start=(t == 0), stop=(t == T - 1))
                    PC.mark(last, b, "Sc")
                if b + 1 < B:
                    VB.wait(eng, b + 1, "Gl")
                    for g in range(5):
                        if g < 2:
                            VW.wait(eng, c, f"jw{g}")
                        VM.wait(eng, b, f"s{g}")
                        expand(b + 1, g)
            general()


_INS = ["x", "src", "dst", "edge_weight", "L0_gnn_W_self", "L0_gnn_W_msg", "L0_gnn_W_Q", "L0_gnn_W_K"]


def kernel(**inputs):
    import numpy as _np
    import concourse.bacc as _bacc
    from concourse import mybir as _mybir
    from concourse.bass_utils import run_bass_kernel_spmd as _run

    nc = _bacc.Bacc("TRN2", target_bir_lowering=False, num_devices=1)
    arrays, args = {}, []
    for name in _INS:
        a = _np.ascontiguousarray(inputs[name])
        arrays[f"in_{name}"] = a
        args.append(nc.dram_tensor(f"in_{name}", a.shape, _mybir.dt.from_np(a.dtype), kind="ExternalInput").ap())
    args.append(nc.dram_tensor("out_0", (12500, 128), _mybir.dt.float32, kind="ExternalOutput").ap())
    gnn_kernel(nc, *args)
    r = _run(nc, [arrays], core_ids=[0])
    return _np.asarray(r.results[0]["out_0"])
```
